# Optimizing a Trainium2 kernel written in Bass

```python
import numpy as np
import jax
import jax.numpy as jnp

def _softmax(x, axis=-1):
    return jax.nn.softmax(x, axis=axis)

def _gelu(x):
    return jax.nn.gelu(x, approximate=True)

def _silu(x):
    return jax.nn.silu(x)

def _sigmoid(x):
    return jax.nn.sigmoid(x)

def _layernorm(x, axis=-1, eps=1e-05):
    m = jnp.mean(x, axis=axis, keepdims=True)
    v = jnp.var(x, axis=axis, keepdims=True)
    return (x - m) / jnp.sqrt(v + eps)

def _scatter_add(tgt, idx, src, axis=0):
    return tgt.at[idx].add(src)

def _segment_sum(src, seg, n):
    return jax.ops.segment_sum(src, seg, n)
kernel_name = 'mk_gnn_resnorm_d2_gnn_r64_8dbc57'

def setup_inputs(seed: int=0):
    np.random.seed(seed)
    _w = jnp.asarray

    def _rec_inputs():
        import jax
        import jax.numpy as jnp
        _gk = jax.random.key(seed)
        x = -0.000202 + 1 * jax.random.normal(jax.random.fold_in(_gk, 1), (100000, 64), jnp.float32)
        src = jax.random.randint(jax.random.fold_in(_gk, 2), (25000,), 0, 100000, jnp.int32)
        dst = jax.random.randint(jax.random.fold_in(_gk, 3), (25000,), 0, 100000, jnp.int32)
        _o = jnp.argsort(dst, stable=True)
        src = src[_o]
        dst = dst[_o]
        return (x, src, dst)
    x, src, dst = _rec_inputs()

    def _L0_gnn_setup():
        import jax, jax.numpy as jnp
        import numpy as np
        N_NODES = 100000
        N_EDGES = 50000
        D = 64
        L = 2
        key = jax.random.key(seed)
        ks = jax.random.split(key, 7)
        x = jax.random.normal(ks[0], (N_NODES, D), dtype=jnp.float32)
        src = jax.random.randint(ks[1], (N_EDGES,), 0, N_NODES, dtype=jnp.int32)
        dst = jax.random.randint(ks[2], (N_EDGES,), 0, N_NODES, dtype=jnp.int32)
        s = 1.0 / np.sqrt(D)
        W1 = jax.random.uniform(ks[3], (L, D, D), jnp.float32, -s, s)
        b1 = jax.random.uniform(ks[4], (L, D), jnp.float32, -s, s)
        W2 = jax.random.uniform(ks[5], (L, D, D), jnp.float32, -s, s)
        b2 = jax.random.uniform(ks[6], (L, D), jnp.float32, -s, s)
        return {'x': x, 'src': src, 'dst': dst, 'W1': W1, 'b1': b1, 'W2': W2, 'b2': b2}
    _L0_gnn_all = _L0_gnn_setup()
    _L0_gnn_in = {k: v for k, v in _L0_gnn_all.items() if k in ('W1', 'b1', 'W2', 'b2')}
    del _L0_gnn_all

    def _L1_gnn_setup():
        import jax, jax.numpy as jnp
        import numpy as np
        N_NODES = 50000
        N_EDGES = 12500
        D = 64
        HID = 128

        def _linear_params(key, fan_in, fan_out):
            kw, kb = jax.random.split(key)
            scale = 1.0 / np.sqrt(fan_in)
            W = jax.random.normal(kw, (fan_in, fan_out), dtype=jnp.float32) * scale
            b = jnp.zeros((fan_out,), dtype=jnp.float32)
            return (W, b)
        key = jax.random.key(seed)
        k_h, k_e, k1, k2, k3, k4 = jax.random.split(key, 6)
        h = jax.random.normal(k_h, (N_NODES, D), dtype=jnp.float32)
        edge_index = jax.random.randint(k_e, (2, N_EDGES), 0, N_NODES, dtype=jnp.int32)
        eW1, eb1 = _linear_params(k1, 2 * D, HID)
        eW2, eb2 = _linear_params(k2, HID, D)
        nW1, nb1 = _linear_params(k3, 2 * D, HID)
        nW2, nb2 = _linear_params(k4, HID, D)
        return {'h': h, 'edge_index': edge_index, 'eW1': eW1, 'eb1': eb1, 'eW2': eW2, 'eb2': eb2, 'nW1': nW1, 'nb1': nb1, 'nW2': nW2, 'nb2': nb2}
    _L1_gnn_all = _L1_gnn_setup()
    _L1_gnn_in = {k: v for k, v in _L1_gnn_all.items() if k in ('eW1', 'eb1', 'eW2', 'eb2', 'nW1', 'nb1', 'nW2', 'nb2')}
    del _L1_gnn_all
    return {'x': x, 'src': src, 'dst': dst, 'L0_gnn_W1': _L0_gnn_in['W1'], 'L0_gnn_b1': _L0_gnn_in['b1'], 'L0_gnn_W2': _L0_gnn_in['W2'], 'L0_gnn_b2': _L0_gnn_in['b2'], 'L1_gnn_eW1': _L1_gnn_in['eW1'], 'L1_gnn_eb1': _L1_gnn_in['eb1'], 'L1_gnn_eW2': _L1_gnn_in['eW2'], 'L1_gnn_eb2': _L1_gnn_in['eb2'], 'L1_gnn_nW1': _L1_gnn_in['nW1'], 'L1_gnn_nb1': _L1_gnn_in['nb1'], 'L1_gnn_nW2': _L1_gnn_in['nW2'], 'L1_gnn_nb2': _L1_gnn_in['nb2']}

def reference(x, src, dst, L0_gnn_W1, L0_gnn_b1, L0_gnn_W2, L0_gnn_b2, L1_gnn_eW1, L1_gnn_eb1, L1_gnn_eW2, L1_gnn_eb2, L1_gnn_nW1, L1_gnn_nb1, L1_gnn_nW2, L1_gnn_nb2):
    import jax
    import jax.numpy as jnp

    def _L0_gnn_ref(x, src, dst, W1, b1, W2, b2):
        import jax, jax.numpy as jnp
        import numpy as np
        N_NODES = 100000
        N_EDGES = 50000
        D = 64
        L = 2
        for l in range(L):
            agg = jax.ops.segment_sum(x[src], dst, num_segments=N_NODES)
            h = x + agg
            h = jnp.tanh(h @ W1[l] + b1[l])
            x = h @ W2[l] + b2[l]
        return x

    def _L1_gnn_ref(h, edge_index, eW1, eb1, eW2, eb2, nW1, nb1, nW2, nb2):
        import jax, jax.numpy as jnp
        import numpy as np
        N_NODES = 50000
        N_EDGES = 12500
        D = 64
        HID = 128

        def _linear_params(key, fan_in, fan_out):
            kw, kb = jax.random.split(key)
            scale = 1.0 / np.sqrt(fan_in)
            W = jax.random.normal(kw, (fan_in, fan_out), dtype=jnp.float32) * scale
            b = jnp.zeros((fan_out,), dtype=jnp.float32)
            return (W, b)
        r, c = (edge_index[0], edge_index[1])
        edge_input = jnp.concatenate([h[r], h[c]], axis=1)
        m_ij = jax.nn.relu(jax.nn.relu(edge_input @ eW1 + eb1) @ eW2 + eb2)
        m_i = jax.ops.segment_sum(m_ij, r, num_segments=h.shape[0])
        agg = jnp.concatenate([h, m_i], axis=1)
        h_out = h + (jax.nn.relu(agg @ nW1 + nb1) @ nW2 + nb2)
        return h_out
    edge_index = jnp.stack([src, dst])
    x = _layernorm(x + _L0_gnn_ref(x, src, dst, L0_gnn_W1, L0_gnn_b1, L0_gnn_W2, L0_gnn_b2), axis=-1)
    x = _layernorm(x + _L1_gnn_ref(x, edge_index, L1_gnn_eW1, L1_gnn_eb1, L1_gnn_eW2, L1_gnn_eb2, L1_gnn_nW1, L1_gnn_nb1, L1_gnn_nW2, L1_gnn_nb2), axis=-1)
    return x

_drawn_inputs = setup_inputs


def setup_inputs(seed=0):
    import zlib

    import numpy as np

    out = dict(_drawn_inputs(seed))
    spreads = {'L1_gnn_eb1': (0.0, 0.8),
     'L1_gnn_eb2': (0.0, 0.8),
     'L1_gnn_nb1': (0.0, 0.1),
     'L1_gnn_nb2': (0.0, 0.1)}
    factors = {}
    for name, (base, spread) in spreads.items():
        noise = np.random.default_rng([zlib.crc32(name.encode()), seed]).standard_normal(out[name].shape)
        drawn = base * np.exp(spread * noise) if base else spread * noise
        out[name] = jnp.asarray(drawn.astype(out[name].dtype))
    for name, factor in factors.items():
        out[name] = (out[name] * factor).astype(out[name].dtype)
    return out
```

```python
import concourse.bass as bass
from concourse import mybir
from contextlib import ExitStack

N = 100000
D = 64
E = 25000
HID = 128
P = 128
TILES = -(-E // P)
LAST = E - (TILES - 1) * P
G = 2
STEPS = TILES // G
ROWS = 8
CHUNK = P * ROWS
TABLE = STEPS * CHUNK
PAD_ROW = N + P
LN_EPS = 1e-5
ZCOLS = 56 * D
ZDMAS = TABLE * D // (P * ZCOLS)
assert STEPS == -(-N // CHUNK) and TILES % G == 0 and TABLE >= N + G * P and ZDMAS * P * ZCOLS == TABLE * D

HEAD, TAIL = 6, 94


class At:

    def __init__(self, i, c):
        self.i, self.c, self.fixed = i, c, isinstance(i, int)
        self.slot = c % 2

    def plus(self, d):
        return At(self.i, self.c + d)

    @property
    def k(self):
        return self.i * 2 + self.c

    @property
    def turn(self):
        return self.i + (self.c // 2 + 1)

    def exists(self):
        return not self.fixed or 0 <= self.c < STEPS

    def after(self, n):
        return not self.fixed or self.c >= n

    def last(self):
        return self.fixed and self.c == STEPS - 1

    def start(self):
        return N - CHUNK if self.last() else self.k * CHUNK


def run_steps(eng, step, before=0, after=0):
    for t in range(-before, HEAD):
        step(At(0, t))
    with eng.Fori(HEAD // 2, TAIL // 2) as i:
        step(At(i, 0))
        step(At(i, 1))
    for t in range(TAIL, STEPS + after):
        step(At(0, t))


def gnn_kernel(nc, x, src, dst, W1, b1, W2, b2, eW1, eb1, eW2, eb2, nW1, nb1, nW2, nb2, out):
    f32, i32 = mybir.dt.float32, mybir.dt.int32
    ALU = mybir.AluOpType
    ACT = mybir.ActivationFunctionType
    AX = mybir.AxisListType.X

    with ExitStack() as ctx:
        def sb(name, shape, dt=f32):
            return ctx.enter_context(nc.sbuf_tensor(name, shape, dt))

        def sem(name):
            return ctx.enter_context(nc.semaphore(name))

        def pair(name):
            return [sem(f"{name}_{s}") for s in range(2)]

        ctx.enter_context(nc.allow_non_contiguous_dma(reason="bias columns, once"))

        def dram(name, shape, dt=f32):
            return nc.dram_tensor(name, shape, dt, kind="Internal").ap()

        agg0 = dram("agg0", [TABLE, D])
        agg1 = dram("agg1", [TABLE, D])
        msum = dram("msum", [TABLE, D])
        x1T = dram("x1T", [STEPS, P, 512])
        h = dram("h", [N, D])
        rows_src = dram("rows_src", [TILES, P], i32)
        rows_dst = dram("rows_dst", [TILES, P], i32)

        ident = sb("ident", [P, P])
        before = sb("before", [P, G, G * P])
        zeros = sb("zeros", [P, ZCOLS])
        mhalf = sb("mhalf", [P, ROWS])
        w1bd = [sb(f"w1bd{l}", [P, P]) for l in range(2)]
        w2bd = [sb(f"w2bd{l}", [P, P]) for l in range(2)]
        b1c = sb("b1c", [P, 2])
        b2c = sb("b2c", [P, 1])
        b2r = sb("b2r", [P, 2, D])
        ew1, ew2 = sb("ew1", [2 * D, HID]), sb("ew2", [HID, D])
        nw1, nw2 = sb("nw1", [2 * D, HID]), sb("nw2", [HID, D])
        eb1c, nb1c = sb("eb1c", [HID, 1]), sb("nb1c", [HID, 1])
        eb2r, nb2r = sb("eb2r", [P, D]), sb("nb2r", [P, D])

        idx_rows = {n: sb(f"idx_rows_{n}", [P, 2, P], i32) for n in "sd"}
        idx_rowf = {n: sb(f"idx_rowf_{n}", [P, 2, P]) for n in "sd"}
        col = {n: sb(f"col_{n}", [P, TILES]) for n in "sd"}
        gat = {n: sb(f"gat_{n}", [P, TILES], i32) for n in "sd"}
        away = {n: sb(f"away_{n}", [P, TILES]) for n in "sd"}
        scat_d = sb("scat_d", [P, TILES], i32)
        diff = sb("diff", [P, P], i32)
        sparei = sb("sparei", [P, G], i32)
        spare = sb("spare", [P, G])

        rowbc = sb("rowbc", [P, 2, G * P], i32)
        eq = sb("eq", [P, 2, G, G * P])
        seen = sb("seen", [P, G, G * P])
        cnt = sb("cnt", [P, 2, G])
        move = sb("move", [P, 2, G])
        gidx = sb("gidx", [P, 2, 2, G], i32)
        sidx = sb("sidx", [P, 2, G], i32)
        xs_ring = sb("xs_ring", [P, 2, G, D])
        xs_all = sb("xs_all", [P, TILES, D])
        ye = sb("ye", [P, 2, G, D])
        yeT = sb("yeT", [P, 2, P])
        hidE = sb("hidE", [P, 2, G * P])
        x1e = sb("x1e", [P, 2, G, D])
        pre = sb("pre", [P, 2, G, D])
        vout = sb("vout", [P, 2, G, D])
        he = sb("he", [P, 2, G, 2 * D])
        heT = sb("heT", [P, 2, G * P])

        xin = sb("xin", [P, 2, 512])
        ain = sb("ain", [P, 2, 512])
        tin = sb("tin", [P, 2, 512])
        yd = sb("yd", [P, 2, 512])
        ydT = sb("ydT", [P, 2, 512])
        hd = sb("hd", [P, 2, 512])
        x1o = sb("x1o", [P, 2, 512])
        xb = sb("xb", [P, 2, 512])
        res = sb("res", [P, 2, 512])
        xc = sb("xc", [P, 2, 512])
        sq = sb("sq", [P, 2, 512])
        fin = sb("fin", [P, 2, 512])
        hm = sb("hm", [P, 2, ROWS, 2, D])
        hmT = sb("hmT", [P, 2, 1024])
        hidN = sb("hidN", [P, 2, 1024])
        mean = sb("mean", [P, 2, ROWS])
        rsum = sb("rsum", [P, 2, ROWS])
        ssum = sb("ssum", [P, 2, ROWS])
        veps = sb("veps", [P, 2, ROWS])
        rstd = sb("rstd", [P, 2, ROWS])

        bank = [ctx.enter_context(nc.psum_tensor(f"bank{i}", [P, 512], f32)) for i in range(8)]

        def chunk_of(table, at):
            return table[bass.ds(at.start(), CHUNK), :].rearrange("(p r) d -> p (r d)", p=P)

        def group_rows(rows, at):
            return rows[bass.ds(at.k * G, G), :].rearrange("t e -> (t e)").partition_broadcast(P)

        def tiles(table, at):
            return table[:, bass.ds(at.k * G, G)]

        turns = sem("turns")
        zeroed0, zeroed1, zeroedm = sem("zeroed0"), sem("zeroed1"), sem("zeroedm")

        pad_made, idx_in, rows_out, w_clear, w_in = (
            sem(n) for n in ("pad_made", "idx_in", "rows_out", "w_clear", "w_in"))
        iotas, consts, idx_f, idx_T, tab, zeros_made = (
            sem(n) for n in ("iotas", "consts", "idx_f", "idx_T", "tab", "zeros_made"))
        W_DMAS = 24
        lists = {"s": (src, rows_src), "d": (dst, rows_dst)}
        full = (TILES - 1 - P) * P

        with nc.Block() as block:
            @block.gpsimd
            def _(pool):
                for n in "sd":
                    nc.gpsimd.iota(idx_rows[n][:, 1, :], pattern=[[1, P]], base=PAD_ROW,
                                   channel_multiplier=0).then_inc(pad_made, 1)
                nc.gpsimd.iota(diff[:, :], pattern=[[1, P]], base=0, channel_multiplier=-1).then_inc(iotas, 1)
                nc.gpsimd.iota(sparei[:, :], pattern=[[P, G]], base=N, channel_multiplier=1).then_inc(iotas, 1)

            @block.sync
            def _(sp):
                sp.wait_ge(pad_made, 2)
                for n in "sd":
                    lst = lists[n][0]
                    sp.dma_start(idx_rows[n][:, 0, :],
                                 lst[0:P * P].rearrange("(t e) -> t e", e=P)).then_inc(idx_in, 16)
                    sp.dma_start(idx_rows[n][0:TILES - 1 - P, 1, :],
                                 lst[P * P:P * P + full].rearrange("(t e) -> t e", e=P)).then_inc(idx_in, 16)
                    sp.dma_start(idx_rows[n][TILES - 1 - P:TILES - P, 1, 0:LAST],
                                 lst[E - LAST:E].rearrange("(t e) -> t e", e=LAST)).then_inc(idx_in, 16)
                sp.wait_ge(w_clear, 4)
                for l in range(2):
                    for q in range(2):
                        a = slice(q * D, (q + 1) * D)
                        sp.dma_start(w1bd[l][a, a], W1[l, :, :]).then_inc(w_in, 16)
                        sp.dma_start(w2bd[l][a, a], W2[l, :, :]).then_inc(w_in, 16)
                        sp.dma_start(b1c[a, l:l + 1], b1[l, :].rearrange("(d o) -> d o", o=1)).then_inc(w_in, 16)
                    sp.dma_start(b2r[:, l, :], b2[l, :].partition_broadcast(P)).then_inc(w_in, 16)
                for q in range(2):
                    sp.dma_start(b2c[q * D:(q + 1) * D, :],
                                 b2[0, :].rearrange("(d o) -> d o", o=1)).then_inc(w_in, 16)
                for to, of in ((ew1, eW1), (ew2, eW2), (nw1, nW1), (nw2, nW2)):
                    sp.dma_start(to[:, :], of).then_inc(w_in, 16)
                for to, of in ((eb1c, eb1), (nb1c, nb1)):
                    sp.dma_start(to[:, :], of.rearrange("(d o) -> d o", o=1)).then_inc(w_in, 16)
                for to, of in ((eb2r, eb2), (nb2r, nb2)):
                    sp.dma_start(to[:, :], of.partition_broadcast(P)).then_inc(w_in, 16)
                sp.wait_ge(idx_in, 96)
                for n in "sd":
                    rows = lists[n][1]
                    sp.dma_start(rows[0:P, :], idx_rows[n][:, 0, :]).then_inc(rows_out, 16)
                    sp.dma_start(rows[P:TILES, :], idx_rows[n][0:TILES - P, 1, :]).then_inc(rows_out, 16)
                sp.wait_ge(rows_out, 64)
                sp.wait_ge(w_in, 16 * W_DMAS)

            @block.scalar
            def _(act):
                act.wait_ge(zeros_made, 1)
                for table, done in ((agg0, zeroed0), (agg1, zeroed1), (msum, zeroedm)):
                    flat = table.rearrange("(z p r) d -> z p (r d)", z=ZDMAS, p=P)
                    for z in range(ZDMAS):
                        act.dma_start(flat[z, :, :], zeros[:, :]).then_inc(done, 16)

            @block.vector
            def _(dve):
                nc.vector.memset(zeros[:, :], 0.0).then_inc(zeros_made, 1)
                for w in (*w1bd, *w2bd):
                    nc.vector.memset(w[:, :], 0.0).then_inc(w_clear, 1)
                nc.vector.memset(mhalf[:, :], -0.5)
                nc.vector.memset(before[:, 0, P:2 * P], 0.0)
                nc.vector.memset(before[:, 1, 0:P], 1.0)
                dve.wait_ge(iotas, 2)
                nc.vector.tensor_scalar(ident[:, :], diff[:, :], 0.0, None, ALU.is_equal).then_inc(consts, 1)
                nc.vector.tensor_scalar(before[:, 0, 0:P], diff[:, :], 0.0, None, ALU.is_lt)
                nc.vector.tensor_scalar(before[:, 1, P:2 * P], diff[:, :], 0.0, None, ALU.is_lt)
                nc.vector.tensor_copy(spare[:, :], sparei[:, :]).then_inc(tab, 1)
                dve.wait_ge(idx_in, 96)
                for n in "sd":
                    nc.vector.tensor_copy(idx_rowf[n][:, :, :], idx_rows[n][:, :, :]).then_inc(idx_f, 1)
                for m, n in enumerate("sd"):
                    dve.wait_ge(idx_T, m + 1)
                    nc.vector.tensor_copy(col[n][:, 0:P], bank[2 * m][:, 0:P])
                    nc.vector.tensor_copy(col[n][:, P:TILES], bank[2 * m + 1][:, 0:TILES - P]).then_inc(tab, 1)
                    dve.wait_ge(tab, m + 2)
                    nc.vector.tensor_scalar(gat[n][:, :], col[n][:, :], float(N - 1), None, ALU.min)
                    nc.vector.tensor_tensor(away[n][:, :].rearrange("p (g t) -> p g t", t=G),
                                            spare[:, :].unsqueeze(1).to_broadcast([P, STEPS, G]),
                                            col[n][:, :].rearrange("p (g t) -> p g t", t=G), ALU.subtract)

            @block.tensor
            def _(pe):
                pe.wait_ge(consts, 1)
                for m, n in enumerate("sd"):
                    pe.wait_ge(idx_f, m + 1)
                    for part in range(2):
                        last = nc.tensor.transpose(bank[2 * m + part][:, 0:P], idx_rowf[n][:, part, :], ident[:, :])
                    last.then_inc(idx_T, 1)

        def equal_pairs(dve, at, n, rows_in, sums_done, eq_ready):
            if at.after(2):
                dve.wait_ge(sums_done, at.k - 1)
            for t in range(G):
                last = nc.vector.tensor_scalar(eq[:, at.slot, t, :], rowbc[:, at.slot, :],
                                               col[n][:, bass.ds(at.k * G + t, 1)], None, ALU.is_equal)
            last.then_inc(eq_ready, 1)

        def scatter_rows(dve, at, n, cnt_done, move_done):
            for t in range(G):
                last = nc.vector.scalar_tensor_tensor(
                    out=seen[:, t, :], in0=rowbc[:, at.slot, :], scalar=col[n][:, bass.ds(at.k * G + t, 1)],
                    in1=before[:, t, :], op0=ALU.is_equal, op1=ALU.mult, accum_out=cnt[:, at.slot, t:t + 1])
            last.then_inc(cnt_done, 1)
            dve.wait_ge(cnt_done, at.k + 1)
            nc.vector.scalar_tensor_tensor(out=move[:, at.slot, :], in0=cnt[:, at.slot, :], scalar=1.0,
                                           in1=tiles(away[n], at), op0=ALU.min, op1=ALU.mult).then_inc(move_done, 1)
            dve.wait_ge(move_done, at.k + 1)

        def group_sums(at, psum, values):
            for j in range(G):
                for t in range(G):
                    last = nc.tensor.matmul(psum[:, j * D:(j + 1) * D], eq[:, at.slot, t, j * P:(j + 1) * P],
                                            values[:, at.slot, t, :], start=(t == 0), stop=(t == G - 1))
            return last

        def add_group(pool, at, table, v_ready, rows_ready, added, zeroed):
            if at.fixed and at.c == 0:
                pool.wait_ge(zeroed, 16 * ZDMAS)
            pool.wait_ge(v_ready, at.k + 1)
            pool.wait_ge(rows_ready, at.k + 1)
            if at.after(1):
                pool.wait_ge(added, at.k * (16 * G))
            carry_waits(pool)
            for t in range(G):
                nc.gpsimd.indirect_dma_start(
                    table, bass.IndirectOffsetOnAxis(ap=sidx[:, at.slot, t:t + 1], axis=0),
                    vout[:, at.slot, t, :], None, compute_op=ALU.add).then_inc(added, 16)

        def carry_waits(pool):
            pool.sem_inc(turns, 1)

        def gather_group(pool, at, table, to, list_slot, landed):
            carry_waits(pool)
            for t in range(G):
                nc.gpsimd.indirect_dma_start(
                    to[:, t, :], None, table,
                    bass.IndirectOffsetOnAxis(ap=gidx[:, at.slot, list_slot, t:t + 1], axis=0)).then_inc(landed, 16)

        rows1, xs_in = pair("rows1"), pair("xs_in")
        gidx1, xs_kept, eq1, cnt1, move1, sidx1, sums1, v1, added0 = (
            sem(n) for n in ("gidx1", "xs_kept", "eq1", "cnt1", "move1", "sidx1", "sums1", "v1", "added0"))

        with nc.Block() as block:
            @block.sync
            def _(sp):
                def step(t):
                    a = t.plus(2)
                    if a.exists():
                        if a.after(2):
                            sp.wait_ge(eq1, a.k - 1)
                        sp.dma_start(rowbc[:, a.slot, :], group_rows(rows_dst, a)).then_inc(rows1[a.slot], 16)
                run_steps(sp, step, before=2)

            @block.gpsimd
            def _(pool):
                def step(t):
                    a = t.plus(2)
                    if a.exists():
                        pool.wait_ge(gidx1, a.k + 1)
                        if a.after(2):
                            pool.wait_ge(xs_kept, a.k - 1)
                            pool.wait_ge(sums1, a.k - 1)
                        gather_group(pool, a, x, xs_ring[:, a.slot, :, :], 0, xs_in[a.slot])
                    if t.exists():
                        add_group(pool, t, agg0, v1, sidx1, added0, zeroed0)
                run_steps(pool, step, before=2)
                pool.wait_ge(added0, 16 * TILES)

            @block.scalar
            def _(act):
                def step(t):
                    a = t.plus(2)
                    if t.exists():
                        act.wait_ge(xs_in[t.slot], t.turn * (16 * G))
                    if a.exists():
                        nc.scalar.copy(gidx[:, a.slot, 0, :], tiles(gat["s"], a)).then_inc(gidx1, 1)
                    if t.exists():
                        nc.scalar.copy(xs_all[:, bass.ds(t.k * G, G), :], xs_ring[:, t.slot, :, :]).then_inc(xs_kept, 1)
                        act.wait_ge(sums1, t.k + 1)
                        if t.after(2):
                            act.wait_ge(added0, (t.k - 1) * (16 * G))
                        nc.scalar.copy(vout[:, t.slot, :, :], bank[t.slot][:, 0:P]
                                       .rearrange("p (t d) -> p t d", d=D)).then_inc(v1, 1)
                run_steps(act, step, before=2)

            @block.vector
            def _(dve):
                def step(t):
                    dve.wait_ge(rows1[t.slot], t.turn * 16)
                    scatter_rows(dve, t, "d", cnt1, move1)
                    nc.vector.tensor_tensor(tiles(scat_d, t), move[:, t.slot, :], tiles(col["d"], t), ALU.add)
                    if t.after(2):
                        dve.wait_ge(added0, (t.k - 1) * (16 * G))
                    nc.vector.tensor_tensor(sidx[:, t.slot, :], move[:, t.slot, :], tiles(col["d"], t),
                                            ALU.add).then_inc(sidx1, 1)
                    equal_pairs(dve, t, "d", rows1, sums1, eq1)
                run_steps(dve, step)

            @block.tensor
            def _(pe):
                def step(t):
                    pe.wait_ge(eq1, t.k + 1)
                    pe.wait_ge(xs_in[t.slot], t.turn * (16 * G))
                    if t.after(2):
                        pe.wait_ge(v1, t.k - 1)
                    group_sums(t, bank[t.slot], xs_ring).then_inc(sums1, 1)
                run_steps(pe, step)

        rows2, ag_in, xd_in, x1_out = pair("rows2"), pair("ag_in"), pair("xd_in"), pair("x1_out")
        (gidx2, sidx2, ye2, yeT_ps, yeT2, hide_ps, hide2, x1e_ps, x1e2, eq2, sums2, v2, added1,
         yd2, ydT_ps, ydT2, hd_ps, hd2, x1_ps, x1_made) = (
            sem(n) for n in ("gidx2", "sidx2", "ye2", "yeT_ps", "yeT2", "hide_ps", "hide2", "x1e_ps", "x1e2",
                             "eq2", "sums2", "v2", "added1", "yd2", "ydT_ps", "ydT2", "hd_ps", "hd2",
                             "x1_ps", "x1_made"))

        with nc.Block() as block:
            @block.sync
            def _(sp):
                def step(t):
                    a = t.plus(2)
                    if a.exists():
                        if a.after(2):
                            sp.wait_ge(eq2, a.k - 1)
                        sp.dma_start(rowbc[:, a.slot, :], group_rows(rows_dst, a)).then_inc(rows2[a.slot], 16)
                        if a.after(2):
                            sp.wait_ge(yd2, a.k - 1)
                        sp.dma_start(xin[:, a.slot, :], chunk_of(x, a)).then_inc(xd_in[a.slot], 16)
                        sp.dma_start(ain[:, a.slot, :], chunk_of(agg0, a)).then_inc(xd_in[a.slot], 16)
                    if t.exists():
                        sp.wait_ge(x1_made, t.k + 1)
                        sp.dma_start(x1T[bass.ds(t.k, 1), :, :].rearrange("o p n -> (o p) n"),
                                     x1o[:, t.slot, :]).then_inc(x1_out[t.slot], 16)
                run_steps(sp, step, before=2)
                for s in range(2):
                    sp.wait_ge(x1_out[s], 16 * STEPS // 2)

            @block.gpsimd
            def _(pool):
                def step(t):
                    a = t.plus(2)
                    if a.exists():
                        pool.wait_ge(gidx2, a.k + 1)
                        if a.after(2):
                            pool.wait_ge(ye2, a.k - 1)
                        gather_group(pool, a, agg0, xs_ring[:, a.slot, :, :], 0, ag_in[a.slot])
                    if t.exists():
                        add_group(pool, t, agg1, v2, sidx2, added1, zeroed1)
                run_steps(pool, step, before=2)
                pool.wait_ge(added1, 16 * TILES)

            @block.scalar
            def _(act):
                def step(t):
                    a = t.plus(2)
                    if t.exists():
                        act.wait_ge(ag_in[t.slot], t.turn * (16 * G))
                    if a.exists():
                        nc.scalar.copy(gidx[:, a.slot, 0, :], tiles(gat["s"], a)).then_inc(gidx2, 1)
                    if not t.exists():
                        return
                    if t.after(2):
                        act.wait_ge(added1, (t.k - 1) * (16 * G))
                    nc.scalar.copy(sidx[:, t.slot, :], tiles(scat_d, t)).then_inc(sidx2, 1)
                    act.wait_ge(hide_ps, t.k + 1)
                    nc.scalar.activation(hidE[:, t.slot, 0:P], bank[1][:, 0:P], ACT.Tanh,
                                         bias=b1c[:, 0:1]).then_inc(hide2, 1)
                    act.wait_ge(hd_ps, t.k + 1)
                    nc.scalar.activation(hd[:, t.slot, :], bank[5][:, :], ACT.Tanh, bias=b1c[:, 0:1]).then_inc(hd2, 1)
                    act.wait_ge(x1_ps, t.k + 1)
                    if t.after(2):
                        act.wait_ge(x1_out[t.slot], (t.turn - 1) * 16)
                    nc.scalar.activation(x1o[:, t.slot, :], bank[6][:, :], ACT.Identity,
                                         bias=b2c[:, 0:1]).then_inc(x1_made, 1)
                    act.wait_ge(sums2, t.k + 1)
                    nc.scalar.copy(vout[:, t.slot, :, :], bank[3][:, 0:P]
                                   .rearrange("p (t d) -> p t d", d=D)).then_inc(v2, 1)
                run_steps(act, step, before=2)

            @block.vector
            def _(dve):
                def step(t):
                    dve.wait_ge(ag_in[t.slot], t.turn * (16 * G))
                    if t.after(2):
                        dve.wait_ge(yeT_ps, t.k - 1)
                    nc.vector.tensor_tensor(ye[:, t.slot, :, :], xs_all[:, bass.ds(t.k * G, G), :],
                                            xs_ring[:, t.slot, :, :], ALU.add).then_inc(ye2, 1)
                    dve.wait_ge(xd_in[t.slot], t.turn * 32)
                    if t.after(2):
                        dve.wait_ge(ydT_ps, t.k - 1)
                    nc.vector.tensor_tensor(yd[:, t.slot, :], xin[:, t.slot, :], ain[:, t.slot, :],
                                            ALU.add).then_inc(yd2, 1)
                    dve.wait_ge(yeT_ps, t.k + 1)
                    nc.vector.tensor_copy(yeT[:, t.slot, :], bank[0][:, 0:P]).then_inc(yeT2, 1)
                    dve.wait_ge(ydT_ps, t.k + 1)
                    nc.vector.tensor_copy(ydT[:, t.slot, :], bank[4][:, :]).then_inc(ydT2, 1)
                    dve.wait_ge(rows2[t.slot], t.turn * 16)
                    equal_pairs(dve, t, "d", rows2, sums2, eq2)
                    dve.wait_ge(x1e_ps, t.k + 1)
                    nc.vector.tensor_tensor(x1e[:, t.slot, :, :], bank[2][:, 0:P].rearrange("p (t d) -> p t d", d=D),
                                            b2r[:, 0:1, :].to_broadcast([P, G, D]), ALU.add).then_inc(x1e2, 1)
                run_steps(dve, step)

            @block.tensor
            def _(pe):
                def step(t):
                    pe.wait_ge(ye2, t.k + 1)
                    if t.after(1):
                        pe.wait_ge(yeT2, t.k)
                    nc.tensor.transpose(bank[0][:, 0:P], ye[:, t.slot, :, :].rearrange("p t d -> p (t d)"),
                                        ident[:, :]).then_inc(yeT_ps, 1)
                    pe.wait_ge(yd2, t.k + 1)
                    if t.after(1):
                        pe.wait_ge(ydT2, t.k)
                    for q in range(4):
                        last = nc.tensor.transpose(bank[4][:, q * P:(q + 1) * P],
                                                   yd[:, t.slot, q * P:(q + 1) * P], ident[:, :])
                    last.then_inc(ydT_ps, 1)
                    pe.wait_ge(yeT2, t.k + 1)
                    if t.after(1):
                        pe.wait_ge(hide2, t.k)
                    nc.tensor.matmul(bank[1][:, 0:P], w1bd[0][:, :], yeT[:, t.slot, :],
                                     start=True, stop=True).then_inc(hide_ps, 1)
                    pe.wait_ge(ydT2, t.k + 1)
                    if t.after(1):
                        pe.wait_ge(hd2, t.k)
                    nc.tensor.matmul(bank[5][:, :], w1bd[0][:, :], ydT[:, t.slot, :],
                                     start=True, stop=True).then_inc(hd_ps, 1)
                    pe.wait_ge(hide2, t.k + 1)
                    if t.after(1):
                        pe.wait_ge(x1e2, t.k)
                    nc.tensor.matmul(bank[2][:, 0:P], hidE[:, t.slot, 0:P], w2bd[0][:, :],
                                     start=True, stop=True).then_inc(x1e_ps, 1)
                    pe.wait_ge(hd2, t.k + 1)
                    if t.after(1):
                        pe.wait_ge(x1_made, t.k)
                    nc.tensor.matmul(bank[6][:, :], w2bd[0][:, :], hd[:, t.slot, :],
                                     start=True, stop=True).then_inc(x1_ps, 1)
                    pe.wait_ge(eq2, t.k + 1)
                    pe.wait_ge(x1e2, t.k + 1)
                    if t.after(1):
                        pe.wait_ge(v2, t.k)
                    group_sums(t, bank[3], x1e).then_inc(sums2, 1)
                run_steps(pe, step)

        in3, h_out = pair("in3"), pair("h_out")
        (aT_ps, z3, hz_ps, hz3, o_ps, xb3, res3, rs3, mean3, xc3, sq3, ss3, veps3, rstd3, fin3) = (
            sem(n) for n in ("aT_ps", "z3", "hz_ps", "hz3", "o_ps", "xb3", "res3", "rs3", "mean3", "xc3", "sq3",
                             "ss3", "veps3", "rstd3", "fin3"))

        def by_row(t):
            return t.rearrange("p (r d) -> p r d", d=D)

        def wide(t):
            return t.unsqueeze(2).to_broadcast([P, ROWS, D])

        def row_means(dve, a, rsum_done, mean_done, xc_done):
            dve.wait_ge(mean_done[1], a.k + 1)
            nc.vector.tensor_reduce(rsum[:, a.slot, :], by_row(res[:, a.slot, :]), AX, ALU.add).then_inc(rsum_done, 1)
            dve.wait_ge(rsum_done, a.k + 1)
            if a.after(2):
                dve.wait_ge(xc_done, a.k - 1)
            nc.vector.tensor_scalar(mean[:, a.slot, :], rsum[:, a.slot, :], 1.0 / D, None,
                                    ALU.mult).then_inc(mean_done[0], 1)

        def row_variances(dve, a, sq_done, ss_done, veps_done, rstd_done):
            dve.wait_ge(sq_done, a.k + 1)
            nc.vector.tensor_reduce(ssum[:, a.slot, :], by_row(sq[:, a.slot, :]), AX, ALU.add).then_inc(ss_done, 1)
            dve.wait_ge(ss_done, a.k + 1)
            if a.after(2):
                dve.wait_ge(rstd_done, a.k - 1)
            nc.vector.tensor_scalar(veps[:, a.slot, :], ssum[:, a.slot, :], 1.0 / D, LN_EPS,
                                    ALU.mult, ALU.add).then_inc(veps_done, 1)

        def centre(pool, a, mean_done, sq_done, fin_done, xc_done):
            pool.wait_ge(mean_done, a.k + 1)
            if a.after(2):
                pool.wait_ge(fin_done, a.k - 1)
                pool.wait_ge(sq_done, a.k - 1)
            nc.gpsimd.tensor_tensor(by_row(xc[:, a.slot, :]), by_row(res[:, a.slot, :]),
                                    wide(mean[:, a.slot, :]), ALU.subtract).then_inc(xc_done, 1)

        def scale_rows(pool, a, veps_done, rstd_done, fin_done, stored):
            pool.wait_ge(veps_done, a.k + 1)
            nc.gpsimd.tensor_tensor(rstd[:, a.slot, :], veps[:, a.slot, :], mhalf[:, :],
                                    ALU.pow).then_inc(rstd_done, 1)
            pool.wait_ge(rstd_done, a.k + 1)
            if a.after(2):
                pool.wait_ge(stored[a.slot], (a.turn - 1) * 16)
            nc.gpsimd.tensor_tensor(by_row(fin[:, a.slot, :]), by_row(xc[:, a.slot, :]),
                                    wide(rstd[:, a.slot, :]), ALU.mult).then_inc(fin_done, 1)

        def store_chunk(sp, a, table, fin_done, stored):
            sp.wait_ge(fin_done, a.k + 1)
            if a.last():
                sp.wait_ge(stored[1 - a.slot], 16 * (STEPS // 2))
            sp.dma_start(chunk_of(table, a), fin[:, a.slot, :]).then_inc(stored[a.slot], 16)

        with nc.Block() as block:
            @block.sync
            def _(sp):
                def step(t):
                    a = t.plus(3)
                    if a.exists():
                        if a.after(2):
                            sp.wait_ge(z3, a.k - 1)
                            sp.wait_ge(aT_ps, a.k - 1)
                            sp.wait_ge(xb3, a.k - 1)
                        sp.dma_start(ain[:, a.slot, :], chunk_of(agg1, a)).then_inc(in3[a.slot], 16)
                        sp.dma_start(tin[:, a.slot, :], x1T[bass.ds(a.k, 1), :, :]
                                     .rearrange("o p n -> (o p) n")).then_inc(in3[a.slot], 16)
                        sp.dma_start(xin[:, a.slot, :], chunk_of(x, a)).then_inc(in3[a.slot], 16)
                    a = t.plus(-2)
                    if a.exists():
                        store_chunk(sp, a, h, fin3, h_out)
                run_steps(sp, step, before=3, after=2)
                for s in range(2):
                    sp.wait_ge(h_out[s], 16 * STEPS // 2)

            @block.tensor
            def _(pe):
                def step(t):
                    a = t.plus(1)
                    if a.exists():
                        pe.wait_ge(in3[a.slot], a.turn * 48)
                        if a.after(2):
                            pe.wait_ge(z3, a.k - 1)
                        for q in range(4):
                            last = nc.tensor.transpose(bank[a.slot][:, q * P:(q + 1) * P],
                                                       ain[:, a.slot, q * P:(q + 1) * P], ident[:, :])
                        last.then_inc(aT_ps, 1)
                    if t.exists():
                        pe.wait_ge(z3, t.k + 1)
                        if t.after(2):
                            pe.wait_ge(hz3, t.k - 1)
                        nc.tensor.matmul(bank[2 + t.slot][:, :], w1bd[1][:, :], ydT[:, t.slot, :],
                                         start=True, stop=True).then_inc(hz_ps, 1)
                    a = t.plus(-1)
                    if a.exists():
                        pe.wait_ge(hz3, a.k + 1)
                        if a.after(2):
                            pe.wait_ge(res3, a.k - 1)
                        for q in range(4):
                            last = nc.tensor.matmul(bank[4 + a.slot][:, q * P:(q + 1) * P],
                                                    hd[:, a.slot, q * P:(q + 1) * P], w2bd[1][:, :],
                                                    start=True, stop=True)
                        last.then_inc(o_ps, 1)
                run_steps(pe, step, before=1, after=1)

            @block.scalar
            def _(act):
                def step(t):
                    if t.exists():
                        act.wait_ge(hz_ps, t.k + 1)
                        if t.after(2):
                            act.wait_ge(o_ps, t.k - 1)
                        nc.scalar.activation(hd[:, t.slot, :], bank[2 + t.slot][:, :], ACT.Tanh,
                                             bias=b1c[:, 1:2]).then_inc(hz3, 1)
                    a = t.plus(-1)
                    if a.exists():
                        act.wait_ge(xc3, a.k + 1)
                        if a.after(2):
                            act.wait_ge(ss3, a.k - 1)
                        nc.scalar.activation(sq[:, a.slot, :], xc[:, a.slot, :], ACT.Square).then_inc(sq3, 1)
                run_steps(act, step, after=1)

            @block.vector
            def _(dve):
                def step(t):
                    a = t.plus(1)
                    if a.exists():
                        dve.wait_ge(aT_ps, a.k + 1)
                        dve.wait_ge(in3[a.slot], a.turn * 48)
                        if a.after(2):
                            dve.wait_ge(hz_ps, a.k - 1)
                        nc.vector.tensor_tensor(ydT[:, a.slot, :], bank[a.slot][:, :], tin[:, a.slot, :],
                                                ALU.add).then_inc(z3, 1)
                    a = t.plus(-1)
                    if a.exists():
                        dve.wait_ge(o_ps, a.k + 1)
                        dve.wait_ge(xb3, a.k + 1)
                        if a.after(2):
                            dve.wait_ge(xc3, a.k - 1)
                        nc.vector.tensor_tensor(res[:, a.slot, :], bank[4 + a.slot][:, :], xb[:, a.slot, :],
                                                ALU.add).then_inc(res3, 1)
                        row_means(dve, a, rs3, (mean3, res3), xc3)
                    a = t.plus(-2)
                    if a.exists():
                        row_variances(dve, a, sq3, ss3, veps3, rstd3)
                run_steps(dve, step, before=1, after=2)

            @block.gpsimd
            def _(pool):
                def step(t):
                    if t.exists():
                        pool.wait_ge(in3[t.slot], t.turn * 48)
                        if t.after(2):
                            pool.wait_ge(res3, t.k - 1)
                        nc.gpsimd.tensor_tensor(by_row(xb[:, t.slot, :]), by_row(xin[:, t.slot, :]),
                                                b2r[:, 1:2, :].to_broadcast([P, ROWS, D]), ALU.add).then_inc(xb3, 1)
                    a = t.plus(-1)
                    if a.exists():
                        centre(pool, a, mean3, sq3, fin3, xc3)
                    a = t.plus(-2)
                    if a.exists():
                        scale_rows(pool, a, veps3, rstd3, fin3, h_out)
                run_steps(pool, step, after=2)

        rows4, he_in = pair("rows4"), pair("he_in")
        (gidx4, cnt4, move4, sidx4, heT_ps, heT4, hid_ps, hid4, m_ps, pre4, m4, eq4, sums4, v4, addedm) = (
            sem(n) for n in ("gidx4", "cnt4", "move4", "sidx4", "heT_ps", "heT4", "hid_ps", "hid4", "m_ps", "pre4",
                             "m4", "eq4", "sums4", "v4", "addedm"))

        with nc.Block() as block:
            @block.sync
            def _(sp):
                def step(t):
                    a = t.plus(2)
                    if a.exists():
                        if a.after(2):
                            sp.wait_ge(eq4, a.k - 1)
                        sp.dma_start(rowbc[:, a.slot, :], group_rows(rows_src, a)).then_inc(rows4[a.slot], 16)
                run_steps(sp, step, before=2)

            @block.gpsimd
            def _(pool):
                def step(t):
                    a = t.plus(2)
                    if a.exists():
                        pool.wait_ge(gidx4, 2 * a.k + 2)
                        if a.after(2):
                            pool.wait_ge(heT_ps, a.k - 1)
                        gather_group(pool, a, h, he[:, a.slot, :, 0:D], 0, he_in[a.slot])
                        gather_group(pool, a, h, he[:, a.slot, :, D:2 * D], 1, he_in[a.slot])
                    if t.exists():
                        add_group(pool, t, msum, v4, sidx4, addedm, zeroedm)
                run_steps(pool, step, before=2)
                pool.wait_ge(addedm, 16 * TILES)

            @block.scalar
            def _(act):
                def step(t):
                    a = t.plus(2)
                    if t.exists():
                        act.wait_ge(he_in[t.slot], t.turn * (32 * G))
                    if a.exists():
                        for m, n in enumerate("sd"):
                            nc.scalar.copy(gidx[:, a.slot, m, :], tiles(gat[n], a)).then_inc(gidx4, 1)
                    if not t.exists():
                        return
                    act.wait_ge(hid_ps, t.k + 1)
                    if t.after(2):
                        act.wait_ge(m_ps, t.k - 1)
                    nc.scalar.activation(hidE[:, t.slot, :], bank[2 + t.slot][:, 0:G * P], ACT.Relu,
                                         bias=eb1c[:, 0:1]).then_inc(hid4, 1)
                    act.wait_ge(pre4, t.k + 1)
                    if t.after(2):
                        act.wait_ge(sums4, t.k - 1)
                    nc.scalar.activation(x1e[:, t.slot, :, :], pre[:, t.slot, :, :], ACT.Relu).then_inc(m4, 1)
                    act.wait_ge(sums4, t.k + 1)
                    if t.after(2):
                        act.wait_ge(addedm, (t.k - 1) * (16 * G))
                    nc.scalar.copy(vout[:, t.slot, :, :], bank[6 + t.slot][:, 0:P]
                                   .rearrange("p (t d) -> p t d", d=D)).then_inc(v4, 1)
                run_steps(act, step, before=2)

            @block.vector
            def _(dve):
                def step(t):
                    dve.wait_ge(heT_ps, t.k + 1)
                    if t.after(2):
                        dve.wait_ge(hid_ps, t.k - 1)
                    nc.vector.tensor_copy(heT[:, t.slot, :], bank[t.slot][:, 0:G * P]).then_inc(heT4, 1)
                    dve.wait_ge(rows4[t.slot], t.turn * 16)
                    scatter_rows(dve, t, "s", cnt4, move4)
                    if t.after(2):
                        dve.wait_ge(addedm, (t.k - 1) * (16 * G))
                    nc.vector.tensor_tensor(sidx[:, t.slot, :], move[:, t.slot, :], tiles(col["s"], t),
                                            ALU.add).then_inc(sidx4, 1)
                    equal_pairs(dve, t, "s", rows4, sums4, eq4)
                    dve.wait_ge(m_ps, t.k + 1)
                    if t.after(2):
                        dve.wait_ge(m4, t.k - 1)
                    nc.vector.tensor_tensor(pre[:, t.slot, :, :], bank[4 + t.slot][:, 0:P]
                                            .rearrange("p (t d) -> p t d", d=D),
                                            eb2r[:, :].unsqueeze(1).to_broadcast([P, G, D]), ALU.add).then_inc(pre4, 1)
                run_steps(dve, step)

            @block.tensor
            def _(pe):
                def step(t):
                    pe.wait_ge(he_in[t.slot], t.turn * (32 * G))
                    if t.after(2):
                        pe.wait_ge(heT4, t.k - 1)
                    for j in range(G):
                        last = nc.tensor.transpose(bank[t.slot][:, j * P:(j + 1) * P], he[:, t.slot, j, :], ident[:, :])
                    last.then_inc(heT_ps, 1)
                    pe.wait_ge(heT4, t.k + 1)
                    if t.after(2):
                        pe.wait_ge(hid4, t.k - 1)
                    nc.tensor.matmul(bank[2 + t.slot][:, 0:G * P], ew1[:, :], heT[:, t.slot, :],
                                     start=True, stop=True).then_inc(hid_ps, 1)
                    pe.wait_ge(hid4, t.k + 1)
                    if t.after(2):
                        pe.wait_ge(pre4, t.k - 1)
                    for j in range(G):
                        last = nc.tensor.matmul(bank[4 + t.slot][:, j * D:(j + 1) * D],
                                                hidE[:, t.slot, j * P:(j + 1) * P], ew2[:, :], start=True, stop=True)
                    last.then_inc(m_ps, 1)
                    pe.wait_ge(eq4, t.k + 1)
                    pe.wait_ge(m4, t.k + 1)
                    if t.after(2):
                        pe.wait_ge(v4, t.k - 1)
                    group_sums(t, bank[6 + t.slot], x1e).then_inc(sums4, 1)
                run_steps(pe, step)

        in5, y_out = pair("in5"), pair("y_out")
        hmT_ps, hmT5, hn_ps, hn5 = pair("hmT_ps"), pair("hmT5"), pair("hn_ps"), pair("hn5")
        (on_ps, hb5, res5, rs5, mean5, xc5, sq5, ss5, veps5, rstd5, fin5) = (
            sem(n) for n in ("on_ps", "hb5", "res5", "rs5", "mean5", "xc5", "sq5", "ss5", "veps5", "rstd5",
                             "fin5"))

        with nc.Block() as block:
            @block.sync
            def _(sp):
                def step(t):
                    a = t.plus(3)
                    if a.exists():
                        if a.after(2):
                            sp.wait_ge(hmT_ps[1], a.k - 1)
                            sp.wait_ge(hb5, a.k - 1)
                        sp.dma_start(hm[:, a.slot, :, 0, :], by_row(chunk_of(h, a))).then_inc(in5[a.slot], 16)
                        sp.dma_start(hm[:, a.slot, :, 1, :], by_row(chunk_of(msum, a))).then_inc(in5[a.slot], 16)
                    a = t.plus(-2)
                    if a.exists():
                        store_chunk(sp, a, out, fin5, y_out)
                run_steps(sp, step, before=3, after=2)
                for s in range(2):
                    sp.wait_ge(y_out[s], 16 * STEPS // 2)

            @block.tensor
            def _(pe):
                def step(t):
                    for half in range(2):
                        a = t.plus(1)
                        if a.exists():
                            pe.wait_ge(in5[a.slot], a.turn * 32)
                            if a.after(1):
                                pe.wait_ge(hmT5[half], a.k)
                            for q in range(4):
                                r = 4 * half + q
                                last = nc.tensor.transpose(bank[half][:, q * P:(q + 1) * P],
                                                           hm[:, a.slot, r, :, :].rearrange("p m d -> p (m d)"), ident[:, :])
                            last.then_inc(hmT_ps[half], 1)
                        if t.exists():
                            pe.wait_ge(hmT5[half], t.k + 1)
                            if t.after(1):
                                pe.wait_ge(hn5[half], t.k)
                            nc.tensor.matmul(bank[2 + half][:, :], nw1[:, :],
                                             hmT[:, t.slot, half * 512:(half + 1) * 512],
                                             start=True, stop=True).then_inc(hn_ps[half], 1)
                    a = t.plus(-1)
                    if a.exists():
                        for half in range(2):
                            pe.wait_ge(hn5[half], a.k + 1)
                        if a.after(2):
                            pe.wait_ge(res5, a.k - 1)
                        for r in range(ROWS):
                            last = nc.tensor.matmul(bank[4 + a.slot][:, r * D:(r + 1) * D],
                                                    hidN[:, a.slot, r * P:(r + 1) * P], nw2[:, :],
                                                    start=True, stop=True)
                        last.then_inc(on_ps, 1)
                run_steps(pe, step, before=1, after=1)

            def spread(eng, copy, a, half):
                eng.wait_ge(hmT_ps[half], a.k + 1)
                if a.after(2):
                    eng.wait_ge(hn_ps[half], a.k - 1)
                copy(hmT[:, a.slot, half * 512:(half + 1) * 512], bank[half][:, :]).then_inc(hmT5[half], 1)

            @block.scalar
            def _(act):
                def step(t):
                    a = t.plus(1)
                    if a.exists():
                        spread(act, nc.scalar.copy, a, 0)
                    if t.exists():
                        for half in range(2):
                            act.wait_ge(hn_ps[half], t.k + 1)
                            if t.after(2):
                                act.wait_ge(on_ps, t.k - 1)
                            nc.scalar.activation(hidN[:, t.slot, half * 512:(half + 1) * 512], bank[2 + half][:, :],
                                                 ACT.Relu, bias=nb1c[:, 0:1]).then_inc(hn5[half], 1)
                    a = t.plus(-1)
                    if a.exists():
                        act.wait_ge(xc5, a.k + 1)
                        if a.after(2):
                            act.wait_ge(ss5, a.k - 1)
                        nc.scalar.activation(sq[:, a.slot, :], xc[:, a.slot, :], ACT.Square).then_inc(sq5, 1)
                run_steps(act, step, before=1, after=1)

            @block.vector
            def _(dve):
                def step(t):
                    a = t.plus(1)
                    if a.exists():
                        spread(dve, nc.vector.tensor_copy, a, 1)
                    a = t.plus(-1)
                    if a.exists():
                        dve.wait_ge(on_ps, a.k + 1)
                        dve.wait_ge(hb5, a.k + 1)
                        if a.after(2):
                            dve.wait_ge(xc5, a.k - 1)
                        nc.vector.tensor_tensor(res[:, a.slot, :], bank[4 + a.slot][:, :], xb[:, a.slot, :],
                                                ALU.add).then_inc(res5, 1)
                        row_means(dve, a, rs5, (mean5, res5), xc5)
                    a = t.plus(1)
                    if a.exists():
                        dve.wait_ge(in5[a.slot], a.turn * 32)
                        if a.after(2):
                            dve.wait_ge(res5, a.k - 1)
                        nc.vector.scalar_tensor_tensor(
                            out=by_row(xb[:, a.slot, :]), in0=hm[:, a.slot, :, 0, :], scalar=2.0,
                            in1=nb2r[:, :].unsqueeze(1).to_broadcast([P, ROWS, D]),
                            op0=ALU.mult, op1=ALU.add).then_inc(hb5, 1)
                    a = t.plus(-2)
                    if a.exists():
                        row_variances(dve, a, sq5, ss5, veps5, rstd5)
                run_steps(dve, step, before=1, after=2)

            @block.gpsimd
            def _(pool):
                def step(t):
                    a = t.plus(-1)
                    if a.exists():
                        centre(pool, a, mean5, sq5, fin5, xc5)
                    a = t.plus(-2)
                    if a.exists():
                        scale_rows(pool, a, veps5, rstd5, fin5, y_out)
                run_steps(pool, step, after=2)


_INS = ['x', 'src', 'dst', 'L0_gnn_W1', 'L0_gnn_b1', 'L0_gnn_W2', 'L0_gnn_b2', 'L1_gnn_eW1', 'L1_gnn_eb1',
        'L1_gnn_eW2', 'L1_gnn_eb2', 'L1_gnn_nW1', 'L1_gnn_nb1', 'L1_gnn_nW2', 'L1_gnn_nb2']


def kernel(**inputs):
    import numpy as _np
    import concourse.bacc as _bacc
    from concourse import mybir as _mybir
    from concourse.bass_utils import run_bass_kernel_spmd as _run

    nc = _bacc.Bacc("TRN2", target_bir_lowering=False, num_devices=1)
    arrays, args = {}, []
    for name in _INS:
        a = _np.ascontiguousarray(inputs[name])
        arrays[f"in_{name}_dram"] = a
        args.append(nc.dram_tensor(f"in_{name}_dram", a.shape, _mybir.dt.from_np(a.dtype), kind="ExternalInput").ap())
    args.append(nc.dram_tensor("out_0_dram", (100000, 64), _mybir.dt.float32, kind="ExternalOutput").ap())
    gnn_kernel(nc, *args)
    r = _run(nc, [arrays], core_ids=[0])
    return r.results[0]["out_0_dram"]
```

```python
import concourse.bass as bass
from concourse import mybir
from contextlib import ExitStack

N = 100000
D = 64
E = 25000
HID = 128
P = 128
TILES = -(-E // P)
LAST = E - (TILES - 1) * P
G = 2
STEPS = TILES // G
ROWS = 8
CHUNK = P * ROWS
TABLE = STEPS * CHUNK
PAD_ROW = N + P
LN_EPS = 1e-5
ZCOLS = 56 * D
ZDMAS = TABLE * D // (P * ZCOLS)
assert STEPS == -(-N // CHUNK) and TILES % G == 0 and TABLE >= N + G * P and ZDMAS * P * ZCOLS == TABLE * D

UNROLL = 8
HEAD, TAIL = 8, 88
LOADS = 4
LEAD = 3
DEEP = 8
DEEP_LEAD = 6


class At:

    def __init__(self, i, c):
        self.i, self.c, self.fixed = i, c, isinstance(i, int)
        self.slot = c % 2
        self.load = c % LOADS
        self.deep = c % DEEP

    def plus(self, d):
        return At(self.i, self.c + d)

    @property
    def k(self):
        return self.i * UNROLL + self.c

    @property
    def turn(self):
        return self.i * (UNROLL // 2) + (self.c // 2 + 1)

    @property
    def load_turn(self):
        return self.i * (UNROLL // LOADS) + (self.c // LOADS + 1)

    @property
    def deep_turn(self):
        return self.i * (UNROLL // DEEP) + (self.c // DEEP + 1)

    def exists(self):
        return not self.fixed or 0 <= self.c < STEPS

    def after(self, n):
        return not self.fixed or self.c >= n

    def last(self):
        return self.fixed and self.c == STEPS - 1

    def start(self):
        return N - CHUNK if self.last() else self.k * CHUNK


def run_steps(eng, step, before=0, after=0):
    for t in range(-before, HEAD):
        step(At(0, t))
    with eng.Fori(HEAD // UNROLL, TAIL // UNROLL) as i:
        for c in range(UNROLL):
            step(At(i, c))
    for t in range(TAIL, STEPS + after):
        step(At(0, t))


def gnn_kernel(nc, x, src, dst, W1, b1, W2, b2, eW1, eb1, eW2, eb2, nW1, nb1, nW2, nb2, out):
    f32, i32, bf16 = mybir.dt.float32, mybir.dt.int32, mybir.dt.bfloat16
    ALU = mybir.AluOpType
    ACT = mybir.ActivationFunctionType
    AX = mybir.AxisListType.X

    with ExitStack() as ctx:
        def sb(name, shape, dt=f32):
            return ctx.enter_context(nc.sbuf_tensor(name, shape, dt))

        def sem(name):
            return ctx.enter_context(nc.semaphore(name))

        def ring(name, slots):
            return [sem(f"{name}_{s}") for s in range(slots)]

        ctx.enter_context(nc.allow_non_contiguous_dma(reason="bias columns, once"))

        def dram(name, shape, dt=f32):
            return nc.dram_tensor(name, shape, dt, kind="Internal").ap()

        agg0 = dram("agg0", [TABLE, D])
        agg1 = dram("agg1", [TABLE, D])
        msum = dram("msum", [TABLE, D])
        x1T = dram("x1T", [STEPS, P, 512])
        h = dram("h", [N, D])
        rows_src = dram("rows_src", [TILES, P], i32)
        rows_dst = dram("rows_dst", [TILES, P], i32)

        ident = sb("ident", [P, P])
        before = sb("before", [P, G, G * P])
        zeros = sb("zeros", [P, ZCOLS])
        mhalf = sb("mhalf", [P, ROWS])
        w1bd = [sb(f"w1bd{l}", [P, P]) for l in range(2)]
        w2bd = [sb(f"w2bd{l}", [P, P]) for l in range(2)]
        b1c = sb("b1c", [P, 2])
        b2c = sb("b2c", [P, 1])
        b2r = sb("b2r", [P, D])
        ones = sb("ones", [P, P], bf16)
        b2parts, nb2parts = sb("b2parts", [P, 512], bf16), sb("nb2parts", [P, 512], bf16)
        taken = sb("taken", [1, 2, 3, D])
        rest = sb("rest", [1, 2, 3, D])
        b2row, nb2row = sb("b2row", [1, D]), sb("nb2row", [1, D])
        ew1, ew2 = sb("ew1", [2 * D, HID]), sb("ew2", [HID, D])
        nw1, nw2 = sb("nw1", [2 * D, HID]), sb("nw2", [HID, D])
        eb1c, nb1c = sb("eb1c", [HID, 1]), sb("nb1c", [HID, 1])
        eb2r = sb("eb2r", [P, D])

        idx_rows = {n: sb(f"idx_rows_{n}", [P, 2, P], i32) for n in "sd"}
        idx_rowf = {n: sb(f"idx_rowf_{n}", [P, 2, P]) for n in "sd"}
        col = {n: sb(f"col_{n}", [P, TILES]) for n in "sd"}
        gat = {n: sb(f"gat_{n}", [P, TILES], i32) for n in "sd"}
        away = {n: sb(f"away_{n}", [P, TILES]) for n in "sd"}
        scat_d = sb("scat_d", [P, TILES], i32)
        diff = sb("diff", [P, P], i32)
        sparei = sb("sparei", [P, G], i32)
        spare = sb("spare", [P, G])

        rowbc = sb("rowbc", [P, 2, G * P], i32)
        eq = sb("eq", [P, 2, G, G * P])
        seen = sb("seen", [P, G, G * P])
        cnt = sb("cnt", [P, 2, G])
        move = sb("move", [P, 2, G])
        gidx = sb("gidx", [P, LOADS, 2, G], i32)
        sidx = sb("sidx", [P, 2, G], i32)
        xs_ring = sb("xs_ring", [P, LOADS, G, D])
        xs_all = sb("xs_all", [P, TILES, D])
        ye = sb("ye", [P, 2, G, D])
        yeT = sb("yeT", [P, 2, P])
        hidE = sb("hidE", [P, 2, G * P])
        x1e = sb("x1e", [P, 2, G, D])
        pre = sb("pre", [P, 2, G, D])
        vout = sb("vout", [P, 2, G, D])
        he = sb("he", [P, LOADS, G, 2 * D])
        heT = sb("heT", [P, 2, G * P])

        xin = sb("xin", [P, LOADS, 512])
        ain = sb("ain", [P, LOADS, 512])
        yd = sb("yd", [P, 2, 512])
        ydT = sb("ydT", [P, 2, 512])
        hd = sb("hd", [P, 2, 512])
        x1o = sb("x1o", [P, 2, 512])
        res = sb("res", [P, 2, 512])
        xc = sb("xc", [P, LOADS, 512])
        sq = sb("sq", [P, 2, 512])
        fin = sb("fin", [P, 2, 512])
        room = xs_all[:, :, :].rearrange("p t d -> p (t d)")
        xin3, ain3, tin3 = (room[:, n * DEEP * 512:(n + 1) * DEEP * 512].rearrange("p (s n) -> p s n", s=DEEP)
                            for n in range(3))
        hm = room[:, 0:DEEP * 1024].rearrange("p (s r m d) -> p s r m d", s=DEEP, r=ROWS, m=2)
        hmT = sb("hmT", [P, 2, 1024])
        hidN = sb("hidN", [P, 2, 1024])
        mean = sb("mean", [P, 2, ROWS])
        rsum = sb("rsum", [P, 2, ROWS])
        ssum = sb("ssum", [P, 2, ROWS])
        veps = sb("veps", [P, LOADS, ROWS])
        std, root, square, factor = (sb(n, [P, 2, ROWS]) for n in ("std", "root", "square", "factor"))
        rstd = sb("rstd", [P, 2, ROWS])

        bank = [ctx.enter_context(nc.psum_tensor(f"bank{i}", [P, 512], f32)) for i in range(8)]

        def chunk_of(table, at):
            return table[bass.ds(at.start(), CHUNK), :].rearrange("(p r) d -> p (r d)", p=P)

        def group_rows(rows, at):
            return rows[bass.ds(at.k * G, G), :].rearrange("t e -> (t e)").partition_broadcast(P)

        def tiles(table, at):
            return table[:, bass.ds(at.k * G, G)]

        turns = sem("turns")
        zeroed0, cleared = sem("zeroed0"), sem("cleared")

        pad_made, idx_in, rows_out, w_clear, w_in = (
            sem(n) for n in ("pad_made", "idx_in", "rows_out", "w_clear", "w_in"))
        iotas, consts, idx_f, idx_T, tab, zeros_made, parts, took = (
            sem(n) for n in ("iotas", "consts", "idx_f", "idx_T", "tab", "zeros_made", "parts", "took"))
        W_DMAS = 24
        lists = {"s": (src, rows_src), "d": (dst, rows_dst)}
        full = (TILES - 1 - P) * P

        with nc.Block() as block:
            @block.gpsimd
            def _(pool):
                for n in "sd":
                    nc.gpsimd.iota(idx_rows[n][:, 1, :], pattern=[[1, P]], base=PAD_ROW,
                                   channel_multiplier=0).then_inc(pad_made, 1)
                nc.gpsimd.iota(diff[:, :], pattern=[[1, P]], base=0, channel_multiplier=-1).then_inc(iotas, 1)
                nc.gpsimd.iota(sparei[:, :], pattern=[[P, G]], base=N, channel_multiplier=1).then_inc(iotas, 1)

            @block.sync
            def _(sp):
                sp.wait_ge(pad_made, 2)
                for n in "sd":
                    lst = lists[n][0]
                    sp.dma_start(idx_rows[n][:, 0, :],
                                 lst[0:P * P].rearrange("(t e) -> t e", e=P)).then_inc(idx_in, 16)
                    sp.dma_start(idx_rows[n][0:TILES - 1 - P, 1, :],
                                 lst[P * P:P * P + full].rearrange("(t e) -> t e", e=P)).then_inc(idx_in, 16)
                    sp.dma_start(idx_rows[n][TILES - 1 - P:TILES - P, 1, 0:LAST],
                                 lst[E - LAST:E].rearrange("(t e) -> t e", e=LAST)).then_inc(idx_in, 16)
                sp.wait_ge(w_clear, 4)
                for l in range(2):
                    for q in range(2):
                        a = slice(q * D, (q + 1) * D)
                        sp.dma_start(w1bd[l][a, a], W1[l, :, :]).then_inc(w_in, 16)
                        sp.dma_start(w2bd[l][a, a], W2[l, :, :]).then_inc(w_in, 16)
                        sp.dma_start(b1c[a, l:l + 1], b1[l, :].rearrange("(d o) -> d o", o=1)).then_inc(w_in, 16)
                for q in range(2):
                    sp.dma_start(b2c[q * D:(q + 1) * D, :],
                                 b2[0, :].rearrange("(d o) -> d o", o=1)).then_inc(w_in, 16)
                for to, of in ((ew1, eW1), (ew2, eW2), (nw1, nW1), (nw2, nW2)):
                    sp.dma_start(to[:, :], of).then_inc(w_in, 16)
                for to, of in ((eb1c, eb1), (nb1c, nb1)):
                    sp.dma_start(to[:, :], of.rearrange("(d o) -> d o", o=1)).then_inc(w_in, 16)
                for to, of in ((eb2r, eb2), (b2r, b2[0, :])):
                    sp.dma_start(to[:, :], of.partition_broadcast(P)).then_inc(w_in, 16)
                for to, of in ((b2row, b2[1:2, :]), (nb2row, nb2.unsqueeze(0))):
                    sp.dma_start(to[:, :], of).then_inc(w_in, 16)
                sp.wait_ge(idx_in, 96)
                for n in "sd":
                    rows = lists[n][1]
                    sp.dma_start(rows[0:P, :], idx_rows[n][:, 0, :]).then_inc(rows_out, 16)
                    sp.dma_start(rows[P:TILES, :], idx_rows[n][0:TILES - P, 1, :]).then_inc(rows_out, 16)
                sp.wait_ge(rows_out, 64)
                sp.wait_ge(w_in, 16 * W_DMAS)

            @block.scalar
            def _(act):
                act.wait_ge(zeros_made, 1)
                act.wait_ge(rows_out, 64)
                flat = agg0.rearrange("(z p r) d -> z p (r d)", z=ZDMAS, p=P)
                for z in range(ZDMAS):
                    act.dma_start(flat[z, :, :], zeros[:, :]).then_inc(zeroed0, 16)

            @block.vector
            def _(dve):
                nc.vector.memset(zeros[:, :], 0.0).then_inc(zeros_made, 1)
                for w in (*w1bd, *w2bd):
                    nc.vector.memset(w[:, :], 0.0).then_inc(w_clear, 1)
                nc.vector.memset(mhalf[:, :], -0.5)
                nc.vector.memset(ones[:, :], 1.0)
                nc.vector.memset(b2parts[:, :], 0.0).then_inc(parts, 1)
                nc.vector.memset(nb2parts[:, :], 0.0).then_inc(parts, 1)
                nc.vector.memset(before[:, 0, P:2 * P], 0.0)
                nc.vector.memset(before[:, 1, 0:P], 1.0)
                dve.wait_ge(iotas, 2)
                nc.vector.tensor_scalar(ident[:, :], diff[:, :], 0.0, None, ALU.is_equal).then_inc(consts, 1)
                nc.vector.tensor_scalar(before[:, 0, 0:P], diff[:, :], 0.0, None, ALU.is_lt)
                nc.vector.tensor_scalar(before[:, 1, P:2 * P], diff[:, :], 0.0, None, ALU.is_lt)
                nc.vector.tensor_copy(spare[:, :], sparei[:, :]).then_inc(tab, 1)
                dve.wait_ge(idx_in, 96)
                for n in "sd":
                    nc.vector.tensor_copy(idx_rowf[n][:, :, :], idx_rows[n][:, :, :]).then_inc(idx_f, 1)
                for m, n in enumerate("sd"):
                    dve.wait_ge(idx_T, m + 1)
                    nc.vector.tensor_copy(col[n][:, 0:P], bank[2 * m][:, 0:P])
                    nc.vector.tensor_copy(col[n][:, P:TILES], bank[2 * m + 1][:, 0:TILES - P]).then_inc(tab, 1)
                    dve.wait_ge(tab, m + 2)
                    nc.vector.tensor_scalar(gat[n][:, :], col[n][:, :], float(N - 1), None, ALU.min)
                    nc.vector.tensor_tensor(away[n][:, :].rearrange("p (g t) -> p g t", t=G),
                                            spare[:, :].unsqueeze(1).to_broadcast([P, STEPS, G]),
                                            col[n][:, :].rearrange("p (g t) -> p g t", t=G), ALU.subtract)

                dve.wait_ge(w_in, 16 * W_DMAS)
                for part in range(3):
                    dve.wait_ge(parts, 2 + 4 * part)
                    for m, (row, to) in enumerate(((b2row, b2parts), (nb2row, nb2parts))):
                        of = row[:, :] if part == 0 else rest[:, m, part - 1, :]
                        nc.vector.tensor_copy(to[32 * part:32 * part + 1, :].rearrange("o (r d) -> o r d", d=D),
                                              of.unsqueeze(1).to_broadcast([1, ROWS, D])).then_inc(parts, 1)
                    dve.wait_ge(parts, 4 + 4 * part)
                    for m, (row, to) in enumerate(((b2row, b2parts), (nb2row, nb2parts))):
                        of = row[:, :] if part == 0 else rest[:, m, part - 1, :]
                        nc.vector.tensor_copy(taken[:, m, part, :], to[32 * part:32 * part + 1, 0:D]).then_inc(took, 1)
                        dve.wait_ge(took, 2 * part + m + 1)
                        nc.vector.tensor_tensor(rest[:, m, part, :], of, taken[:, m, part, :],
                                                ALU.subtract).then_inc(parts, 1)

            @block.tensor
            def _(pe):
                pe.wait_ge(consts, 1)
                for m, n in enumerate("sd"):
                    pe.wait_ge(idx_f, m + 1)
                    for part in range(2):
                        last = nc.tensor.transpose(bank[2 * m + part][:, 0:P], idx_rowf[n][:, part, :], ident[:, :])
                    last.then_inc(idx_T, 1)

        def equal_pairs(dve, at, n, rows_in, sums_done, eq_ready):
            if at.after(2):
                dve.wait_ge(sums_done, at.k - 1)
            for t in range(G):
                last = nc.vector.tensor_scalar(eq[:, at.slot, t, :], rowbc[:, at.slot, :],
                                               col[n][:, bass.ds(at.k * G + t, 1)], None, ALU.is_equal)
            last.then_inc(eq_ready, 1)

        def scatter_rows(dve, at, n, cnt_done, move_done):
            for t in range(G):
                last = nc.vector.scalar_tensor_tensor(
                    out=seen[:, t, :], in0=rowbc[:, at.slot, :], scalar=col[n][:, bass.ds(at.k * G + t, 1)],
                    in1=before[:, t, :], op0=ALU.is_equal, op1=ALU.mult, accum_out=cnt[:, at.slot, t:t + 1])
            last.then_inc(cnt_done, 1)
            dve.wait_ge(cnt_done, at.k + 1)
            nc.vector.scalar_tensor_tensor(out=move[:, at.slot, :], in0=cnt[:, at.slot, :], scalar=1.0,
                                           in1=tiles(away[n], at), op0=ALU.min, op1=ALU.mult).then_inc(move_done, 1)
            dve.wait_ge(move_done, at.k + 1)

        def group_sums(at, psum, values):
            for j in range(G):
                for t in range(G):
                    last = nc.tensor.matmul(psum[:, j * D:(j + 1) * D], eq[:, at.slot, t, j * P:(j + 1) * P],
                                            values[:, t, :], start=(t == 0), stop=(t == G - 1))
            return last

        def add_group(pool, at, table, v_ready, rows_ready, added, zeroed):
            if at.fixed and at.c == 0:
                pool.wait_ge(*zeroed)
            pool.wait_ge(v_ready, at.k + 1)
            pool.wait_ge(rows_ready, at.k + 1)
            if at.after(1):
                pool.wait_ge(added, at.k * (16 * G))
            carry_waits(pool)
            for t in range(G):
                nc.gpsimd.indirect_dma_start(
                    table, bass.IndirectOffsetOnAxis(ap=sidx[:, at.slot, t:t + 1], axis=0),
                    vout[:, at.slot, t, :], None, compute_op=ALU.add).then_inc(added, 16)

        def carry_waits(pool):
            pool.sem_inc(turns, 1)

        def gather_group(pool, at, table, to, list_slot, landed):
            carry_waits(pool)
            for t in range(G):
                nc.gpsimd.indirect_dma_start(
                    to[:, t, :], None, table,
                    bass.IndirectOffsetOnAxis(ap=gidx[:, at.load, list_slot, t:t + 1], axis=0)).then_inc(landed, 16)

        rows1, xs_in = ring("rows1", 2), ring("xs_in", LOADS)
        gidx1, xs_kept, eq1, cnt1, move1, sidx1, sums1, v1, added0 = (
            sem(n) for n in ("gidx1", "xs_kept", "eq1", "cnt1", "move1", "sidx1", "sums1", "v1", "added0"))

        with nc.Block() as block:
            @block.sync
            def _(sp):
                def step(t):
                    a = t.plus(2)
                    if a.exists():
                        if a.after(2):
                            sp.wait_ge(eq1, a.k - 1)
                        sp.dma_start(rowbc[:, a.slot, :], group_rows(rows_dst, a)).then_inc(rows1[a.slot], 16)
                    if t.exists():
                        if t.fixed and t.c == 0:
                            sp.wait_ge(zeroed0, 16 * ZDMAS)
                        for table in (agg1, msum):
                            sp.dma_start(table[bass.ds(t.k * CHUNK, CHUNK), :].rearrange("(p r) d -> p (r d)", p=P),
                                         zeros[:, 0:512]).then_inc(cleared, 16)
                run_steps(sp, step, before=2)

            @block.gpsimd
            def _(pool):
                def step(t):
                    a = t.plus(LEAD)
                    if a.exists():
                        pool.wait_ge(gidx1, a.k + 1)
                        if a.after(LOADS):
                            pool.wait_ge(xs_kept, a.k - 3)
                            pool.wait_ge(sums1, a.k - 3)
                        gather_group(pool, a, x, xs_ring[:, a.load, :, :], 0, xs_in[a.load])
                    if t.exists():
                        add_group(pool, t, agg0, v1, sidx1, added0, (zeroed0, 16 * ZDMAS))
                run_steps(pool, step, before=LEAD)
                pool.wait_ge(added0, 16 * TILES)

            @block.scalar
            def _(act):
                def step(t):
                    a = t.plus(LEAD)
                    if a.exists():
                        nc.scalar.copy(gidx[:, a.load, 0, :], tiles(gat["s"], a)).then_inc(gidx1, 1)
                    if t.exists():
                        act.wait_ge(xs_in[t.load], t.load_turn * (16 * G))
                        nc.scalar.copy(xs_all[:, bass.ds(t.k * G, G), :], xs_ring[:, t.load, :, :]).then_inc(xs_kept, 1)
                        act.wait_ge(sums1, t.k + 1)
                        if t.after(2):
                            act.wait_ge(added0, (t.k - 1) * (16 * G))
                        nc.scalar.copy(vout[:, t.slot, :, :], bank[t.slot][:, 0:P]
                                       .rearrange("p (t d) -> p t d", d=D)).then_inc(v1, 1)
                run_steps(act, step, before=LEAD)

            @block.vector
            def _(dve):
                def step(t):
                    dve.wait_ge(rows1[t.slot], t.turn * 16)
                    scatter_rows(dve, t, "d", cnt1, move1)
                    nc.vector.tensor_tensor(tiles(scat_d, t), move[:, t.slot, :], tiles(col["d"], t), ALU.add)
                    if t.after(2):
                        dve.wait_ge(added0, (t.k - 1) * (16 * G))
                    nc.vector.tensor_tensor(sidx[:, t.slot, :], move[:, t.slot, :], tiles(col["d"], t),
                                            ALU.add).then_inc(sidx1, 1)
                    equal_pairs(dve, t, "d", rows1, sums1, eq1)
                run_steps(dve, step)

            @block.tensor
            def _(pe):
                def step(t):
                    pe.wait_ge(eq1, t.k + 1)
                    pe.wait_ge(xs_in[t.load], t.load_turn * (16 * G))
                    if t.after(2):
                        pe.wait_ge(v1, t.k - 1)
                    group_sums(t, bank[t.slot], xs_ring[:, t.load, :, :]).then_inc(sums1, 1)
                run_steps(pe, step)

        rows2, x1_out, ag_in, xd_in = ring("rows2", 2), ring("x1_out", 2), ring("ag_in", LOADS), ring("xd_in", LOADS)
        (gidx2, sidx2, ye2, yeT_ps, yeT2, hide_ps, hide2, x1e_ps, x1e2, eq2, sums2, v2, added1,
         yd2, ydT_ps, ydT2, hd_ps, hd2, x1_ps, x1_made) = (
            sem(n) for n in ("gidx2", "sidx2", "ye2", "yeT_ps", "yeT2", "hide_ps", "hide2", "x1e_ps", "x1e2",
                             "eq2", "sums2", "v2", "added1", "yd2", "ydT_ps", "ydT2", "hd_ps", "hd2",
                             "x1_ps", "x1_made"))

        with nc.Block() as block:
            @block.sync
            def _(sp):
                def step(t):
                    a = t.plus(2)
                    if a.exists():
                        if a.after(2):
                            sp.wait_ge(eq2, a.k - 1)
                        sp.dma_start(rowbc[:, a.slot, :], group_rows(rows_dst, a)).then_inc(rows2[a.slot], 16)
                    a = t.plus(LEAD)
                    if a.exists():
                        if a.after(LOADS):
                            sp.wait_ge(yd2, a.k - 3)
                        sp.dma_start(xin[:, a.load, :], chunk_of(x, a)).then_inc(xd_in[a.load], 16)
                        sp.dma_start(ain[:, a.load, :], chunk_of(agg0, a)).then_inc(xd_in[a.load], 16)
                    if t.exists():
                        sp.wait_ge(x1_made, t.k + 1)
                        sp.dma_start(x1T[bass.ds(t.k, 1), :, :].rearrange("o p n -> (o p) n"),
                                     x1o[:, t.slot, :]).then_inc(x1_out[t.slot], 16)
                run_steps(sp, step, before=LEAD)
                for s in range(2):
                    sp.wait_ge(x1_out[s], 16 * STEPS // 2)

            @block.gpsimd
            def _(pool):
                def step(t):
                    a = t.plus(LEAD)
                    if a.exists():
                        pool.wait_ge(gidx2, a.k + 1)
                        if a.after(LOADS):
                            pool.wait_ge(ye2, a.k - 3)
                        gather_group(pool, a, agg0, xs_ring[:, a.load, :, :], 0, ag_in[a.load])
                    if t.exists():
                        add_group(pool, t, agg1, v2, sidx2, added1, (cleared, 32 * STEPS))
                run_steps(pool, step, before=LEAD)
                pool.wait_ge(added1, 16 * TILES)

            @block.scalar
            def _(act):
                def step(t):
                    a = t.plus(LEAD)
                    if a.exists():
                        if a.after(LOADS):
                            act.wait_ge(ag_in[a.load], (a.load_turn - 1) * (16 * G))
                        nc.scalar.copy(gidx[:, a.load, 0, :], tiles(gat["s"], a)).then_inc(gidx2, 1)
                    if not t.exists():
                        return
                    if t.after(2):
                        act.wait_ge(added1, (t.k - 1) * (16 * G))
                    nc.scalar.copy(sidx[:, t.slot, :], tiles(scat_d, t)).then_inc(sidx2, 1)
                    act.wait_ge(hide_ps, t.k + 1)
                    nc.scalar.activation(hidE[:, t.slot, 0:P], bank[1][:, 0:P], ACT.Tanh,
                                         bias=b1c[:, 0:1]).then_inc(hide2, 1)
                    act.wait_ge(hd_ps, t.k + 1)
                    nc.scalar.activation(hd[:, t.slot, :], bank[5][:, :], ACT.Tanh, bias=b1c[:, 0:1]).then_inc(hd2, 1)
                    act.wait_ge(x1_ps, t.k + 1)
                    if t.after(2):
                        act.wait_ge(x1_out[t.slot], (t.turn - 1) * 16)
                    nc.scalar.activation(x1o[:, t.slot, :], bank[6][:, :], ACT.Identity,
                                         bias=b2c[:, 0:1]).then_inc(x1_made, 1)
                    act.wait_ge(sums2, t.k + 1)
                    nc.scalar.copy(vout[:, t.slot, :, :], bank[3][:, 0:P]
                                   .rearrange("p (t d) -> p t d", d=D)).then_inc(v2, 1)
                run_steps(act, step, before=LEAD)

            @block.vector
            def _(dve):
                def step(t):
                    dve.wait_ge(ag_in[t.load], t.load_turn * (16 * G))
                    if t.after(2):
                        dve.wait_ge(yeT_ps, t.k - 1)
                    nc.vector.tensor_tensor(ye[:, t.slot, :, :], xs_all[:, bass.ds(t.k * G, G), :],
                                            xs_ring[:, t.load, :, :], ALU.add).then_inc(ye2, 1)
                    dve.wait_ge(xd_in[t.load], t.load_turn * 32)
                    if t.after(2):
                        dve.wait_ge(ydT_ps, t.k - 1)
                    nc.vector.tensor_tensor(yd[:, t.slot, :], xin[:, t.load, :], ain[:, t.load, :],
                                            ALU.add).then_inc(yd2, 1)
                    dve.wait_ge(yeT_ps, t.k + 1)
                    nc.vector.tensor_copy(yeT[:, t.slot, :], bank[0][:, 0:P]).then_inc(yeT2, 1)
                    dve.wait_ge(ydT_ps, t.k + 1)
                    nc.vector.tensor_copy(ydT[:, t.slot, :], bank[4][:, :]).then_inc(ydT2, 1)
                    dve.wait_ge(rows2[t.slot], t.turn * 16)
                    equal_pairs(dve, t, "d", rows2, sums2, eq2)
                    dve.wait_ge(x1e_ps, t.k + 1)
                    nc.vector.tensor_tensor(x1e[:, t.slot, :, :], bank[2][:, 0:P].rearrange("p (t d) -> p t d", d=D),
                                            b2r[:, :].unsqueeze(1).to_broadcast([P, G, D]), ALU.add).then_inc(x1e2, 1)
                run_steps(dve, step)

            @block.tensor
            def _(pe):
                def step(t):
                    pe.wait_ge(ye2, t.k + 1)
                    if t.after(1):
                        pe.wait_ge(yeT2, t.k)
                    nc.tensor.transpose(bank[0][:, 0:P], ye[:, t.slot, :, :].rearrange("p t d -> p (t d)"),
                                        ident[:, :]).then_inc(yeT_ps, 1)
                    pe.wait_ge(yd2, t.k + 1)
                    if t.after(1):
                        pe.wait_ge(ydT2, t.k)
                    for q in range(4):
                        last = nc.tensor.transpose(bank[4][:, q * P:(q + 1) * P],
                                                   yd[:, t.slot, q * P:(q + 1) * P], ident[:, :])
                    last.then_inc(ydT_ps, 1)
                    pe.wait_ge(yeT2, t.k + 1)
                    if t.after(1):
                        pe.wait_ge(hide2, t.k)
                    nc.tensor.matmul(bank[1][:, 0:P], w1bd[0][:, :], yeT[:, t.slot, :],
                                     start=True, stop=True).then_inc(hide_ps, 1)
                    pe.wait_ge(ydT2, t.k + 1)
                    if t.after(1):
                        pe.wait_ge(hd2, t.k)
                    nc.tensor.matmul(bank[5][:, :], w1bd[0][:, :], ydT[:, t.slot, :],
                                     start=True, stop=True).then_inc(hd_ps, 1)
                    pe.wait_ge(hide2, t.k + 1)
                    if t.after(1):
                        pe.wait_ge(x1e2, t.k)
                    nc.tensor.matmul(bank[2][:, 0:P], hidE[:, t.slot, 0:P], w2bd[0][:, :],
                                     start=True, stop=True).then_inc(x1e_ps, 1)
                    pe.wait_ge(hd2, t.k + 1)
                    if t.after(1):
                        pe.wait_ge(x1_made, t.k)
                    nc.tensor.matmul(bank[6][:, :], w2bd[0][:, :], hd[:, t.slot, :],
                                     start=True, stop=True).then_inc(x1_ps, 1)
                    pe.wait_ge(eq2, t.k + 1)
                    pe.wait_ge(x1e2, t.k + 1)
                    if t.after(1):
                        pe.wait_ge(v2, t.k)
                    group_sums(t, bank[3], x1e[:, t.slot, :, :]).then_inc(sums2, 1)
                run_steps(pe, step)

        in3, h_out = ring("in3", DEEP), ring("h_out", 2)
        (z_ps, z3, hz_ps, hz3, o_ps, res3, rs3, mean3, xc3, sq3, ss3, veps3, rstd3, fin3) = (
            sem(n) for n in ("z_ps", "z3", "hz_ps", "hz3", "o_ps", "res3", "rs3", "mean3", "xc3", "sq3",
                             "ss3", "veps3", "rstd3", "fin3"))

        def by_row(t):
            return t.rearrange("p (r d) -> p r d", d=D)

        def wide(t):
            return t.unsqueeze(2).to_broadcast([P, ROWS, D])

        def row_sums(dve, a, res_done, rsum_done):
            dve.wait_ge(res_done, a.k + 1)
            nc.vector.tensor_reduce(rsum[:, a.slot, :], by_row(res[:, a.slot, :]), AX, ALU.add).then_inc(rsum_done, 1)

        def row_means(dve, a, rsum_done, mean_done, xc_done):
            dve.wait_ge(rsum_done, a.k + 1)
            if a.after(2):
                dve.wait_ge(xc_done, a.k - 1)
            nc.vector.tensor_scalar(mean[:, a.slot, :], rsum[:, a.slot, :], 1.0 / D, None,
                                    ALU.mult).then_inc(mean_done, 1)

        def square_sums(dve, a, sq_done, ss_done):
            dve.wait_ge(sq_done, a.k + 1)
            nc.vector.tensor_reduce(ssum[:, a.slot, :], by_row(sq[:, a.slot, :]), AX, ALU.add).then_inc(ss_done, 1)

        def row_variances(dve, a, ss_done, veps_done, rstd_done):
            dve.wait_ge(ss_done, a.k + 1)
            if a.after(LOADS):
                dve.wait_ge(rstd_done, a.k - 3)
            nc.vector.tensor_scalar(veps[:, a.load, :], ssum[:, a.slot, :], 1.0 / D, LN_EPS,
                                    ALU.mult, ALU.add).then_inc(veps_done, 1)

        def centre(pool, a, mean_done, sq_done, fin_done, xc_done):
            pool.wait_ge(mean_done, a.k + 1)
            if a.after(LOADS):
                pool.wait_ge(fin_done, a.k - 3)
                pool.wait_ge(sq_done, a.k - 3)
            nc.gpsimd.tensor_tensor(by_row(xc[:, a.load, :]), by_row(res[:, a.slot, :]),
                                    wide(mean[:, a.slot, :]), ALU.subtract).then_inc(xc_done, 1)

        def scale_rows(eng, ops, a, rstd_done, fin_done, stored):
            eng.wait_ge(rstd_done, a.k + 1)
            if a.after(2):
                eng.wait_ge(stored[a.slot], (a.turn - 1) * 16)
            ops.tensor_tensor(by_row(fin[:, a.slot, :]), by_row(xc[:, a.load, :]),
                              wide(rstd[:, a.slot, :]), ALU.mult).then_inc(fin_done, 1)

        def store_chunk(sp, a, table, fin_done, stored):
            sp.wait_ge(fin_done, a.k + 1)
            if a.last():
                sp.wait_ge(stored[1 - a.slot], 16 * (STEPS // 2))
            sp.dma_start(chunk_of(table, a), fin[:, a.slot, :]).then_inc(stored[a.slot], 16)

        with nc.Block() as block:
            @block.sync
            def _(sp):
                def step(t):
                    a = t.plus(DEEP_LEAD)
                    if a.exists():
                        if a.after(DEEP):
                            sp.wait_ge(z3, a.k - DEEP + 1)
                            sp.wait_ge(res3, a.k - DEEP + 1)
                        sp.dma_start(ain3[:, a.deep, :], chunk_of(agg1, a)).then_inc(in3[a.deep], 16)
                        sp.dma_start(tin3[:, a.deep, :], x1T[bass.ds(a.k, 1), :, :]
                                     .rearrange("o p n -> (o p) n")).then_inc(in3[a.deep], 16)
                        sp.dma_start(xin3[:, a.deep, :], chunk_of(x, a)).then_inc(in3[a.deep], 16)
                    a = t.plus(-3)
                    if a.exists():
                        store_chunk(sp, a, h, fin3, h_out)
                run_steps(sp, step, before=DEEP_LEAD, after=3)
                for s in range(2):
                    sp.wait_ge(h_out[s], 16 * STEPS // 2)

            @block.tensor
            def _(pe):
                def step(t):
                    a = t.plus(-1)
                    if a.exists():
                        pe.wait_ge(hz3, a.k + 1)
                        if a.after(2):
                            pe.wait_ge(res3, a.k - 1)
                        nc.tensor.matmul(bank[4 + a.slot][:, :], ones[:, :], b2parts[:, :],
                                         start=True, stop=False)
                        for q in range(4):
                            last = nc.tensor.matmul(bank[4 + a.slot][:, q * P:(q + 1) * P],
                                                    hd[:, a.slot, q * P:(q + 1) * P], w2bd[1][:, :],
                                                    start=False, stop=(q == 3))
                        last.then_inc(o_ps, 1)
                    if t.exists():
                        pe.wait_ge(z3, t.k + 1)
                        if t.after(2):
                            pe.wait_ge(hz3, t.k - 1)
                        nc.tensor.matmul(bank[2 + t.slot][:, :], w1bd[1][:, :], ydT[:, t.slot, :],
                                         start=True, stop=True).then_inc(hz_ps, 1)
                    a = t.plus(2)
                    if a.exists():
                        pe.wait_ge(in3[a.deep], a.deep_turn * 48)
                        if a.after(2):
                            pe.wait_ge(z3, a.k - 1)
                        for q in range(4):
                            last = nc.tensor.transpose(bank[a.slot][:, q * P:(q + 1) * P],
                                                       ain3[:, a.deep, q * P:(q + 1) * P], ident[:, :])
                        last.then_inc(z_ps, 1)
                run_steps(pe, step, before=2, after=1)

            @block.scalar
            def _(act):
                def step(t):
                    if t.exists():
                        act.wait_ge(hz_ps, t.k + 1)
                        if t.after(2):
                            act.wait_ge(o_ps, t.k - 1)
                        nc.scalar.activation(hd[:, t.slot, :], bank[2 + t.slot][:, :], ACT.Tanh,
                                             bias=b1c[:, 1:2]).then_inc(hz3, 1)
                    a = t.plus(-1)
                    if a.exists():
                        act.wait_ge(xc3, a.k + 1)
                        if a.after(2):
                            act.wait_ge(ss3, a.k - 1)
                        nc.scalar.activation(sq[:, a.slot, :], xc[:, a.load, :], ACT.Square).then_inc(sq3, 1)
                run_steps(act, step, after=1)

            @block.vector
            def _(dve):
                def step(t):
                    a = t.plus(1)
                    if a.exists():
                        dve.wait_ge(z_ps, a.k + 1)
                        dve.wait_ge(in3[a.deep], a.deep_turn * 48)
                        if a.after(2):
                            dve.wait_ge(hz_ps, a.k - 1)
                        nc.vector.tensor_tensor(ydT[:, a.slot, :], bank[a.slot][:, :], tin3[:, a.deep, :],
                                                ALU.add).then_inc(z3, 1)
                    a = t.plus(-1)
                    if a.exists():
                        dve.wait_ge(o_ps, a.k + 1)
                        if a.after(2):
                            dve.wait_ge(xc3, a.k - 1)
                        nc.vector.tensor_tensor(res[:, a.slot, :], bank[4 + a.slot][:, :], xin3[:, a.deep, :],
                                                ALU.add).then_inc(res3, 1)
                        row_sums(dve, a, res3, rs3)
                    b = t.plus(-2)
                    if b.exists():
                        square_sums(dve, b, sq3, ss3)
                    if a.exists():
                        row_means(dve, a, rs3, mean3, xc3)
                    c = t.plus(-3)
                    if c.exists():
                        scale_rows(dve, nc.vector, c, rstd3, fin3, h_out)
                    if b.exists():
                        row_variances(dve, b, ss3, veps3, rstd3)
                run_steps(dve, step, before=1, after=3)

            @block.gpsimd
            def _(pool):
                def step(t):
                    a = t.plus(-1)
                    if a.exists():
                        centre(pool, a, mean3, sq3, fin3, xc3)
                    a = t.plus(-2)
                    if a.exists():
                        pool.wait_ge(veps3, a.k + 1)
                        if a.after(2):
                            pool.wait_ge(fin3, a.k - 1)
                        nc.gpsimd.tensor_tensor(rstd[:, a.slot, :], veps[:, a.load, :], mhalf[:, :],
                                                ALU.pow).then_inc(rstd3, 1)
                run_steps(pool, step, after=2)

        rows4, he_in = ring("rows4", 2), ring("he_in", LOADS)
        (gidx4, cnt4, move4, sidx4, heT_ps, heT4, hid_ps, hid4, m_ps, pre4, m4, eq4, sums4, v4, addedm) = (
            sem(n) for n in ("gidx4", "cnt4", "move4", "sidx4", "heT_ps", "heT4", "hid_ps", "hid4", "m_ps", "pre4",
                             "m4", "eq4", "sums4", "v4", "addedm"))

        with nc.Block() as block:
            @block.sync
            def _(sp):
                def step(t):
                    a = t.plus(2)
                    if a.exists():
                        if a.after(2):
                            sp.wait_ge(eq4, a.k - 1)
                        sp.dma_start(rowbc[:, a.slot, :], group_rows(rows_src, a)).then_inc(rows4[a.slot], 16)
                run_steps(sp, step, before=2)

            @block.gpsimd
            def _(pool):
                def step(t):
                    a = t.plus(LEAD)
                    if a.exists():
                        pool.wait_ge(gidx4, 2 * a.k + 2)
                        if a.after(LOADS):
                            pool.wait_ge(heT_ps, a.k - 3)
                        gather_group(pool, a, h, he[:, a.load, :, 0:D], 0, he_in[a.load])
                        gather_group(pool, a, h, he[:, a.load, :, D:2 * D], 1, he_in[a.load])
                    if t.exists():
                        add_group(pool, t, msum, v4, sidx4, addedm, (cleared, 32 * STEPS))
                run_steps(pool, step, before=LEAD)
                pool.wait_ge(addedm, 16 * TILES)

            @block.scalar
            def _(act):
                def step(t):
                    a = t.plus(LEAD)
                    if a.exists():
                        if a.after(LOADS):
                            act.wait_ge(he_in[a.load], (a.load_turn - 1) * (32 * G))
                        for m, n in enumerate("sd"):
                            nc.scalar.copy(gidx[:, a.load, m, :], tiles(gat[n], a)).then_inc(gidx4, 1)
                    if not t.exists():
                        return
                    act.wait_ge(hid_ps, t.k + 1)
                    if t.after(2):
                        act.wait_ge(m_ps, t.k - 1)
                    nc.scalar.activation(hidE[:, t.slot, :], bank[2 + t.slot][:, 0:G * P], ACT.Relu,
                                         bias=eb1c[:, 0:1]).then_inc(hid4, 1)
                    act.wait_ge(pre4, t.k + 1)
                    if t.after(2):
                        act.wait_ge(sums4, t.k - 1)
                    nc.scalar.activation(x1e[:, t.slot, :, :], pre[:, t.slot, :, :], ACT.Relu).then_inc(m4, 1)
                    act.wait_ge(sums4, t.k + 1)
                    if t.after(2):
                        act.wait_ge(addedm, (t.k - 1) * (16 * G))
                    nc.scalar.copy(vout[:, t.slot, :, :], bank[6 + t.slot][:, 0:P]
                                   .rearrange("p (t d) -> p t d", d=D)).then_inc(v4, 1)
                run_steps(act, step, before=LEAD)

            @block.vector
            def _(dve):
                def step(t):
                    dve.wait_ge(heT_ps, t.k + 1)
                    if t.after(2):
                        dve.wait_ge(hid_ps, t.k - 1)
                    nc.vector.tensor_copy(heT[:, t.slot, :], bank[t.slot][:, 0:G * P]).then_inc(heT4, 1)
                    dve.wait_ge(rows4[t.slot], t.turn * 16)
                    scatter_rows(dve, t, "s", cnt4, move4)
                    if t.after(2):
                        dve.wait_ge(addedm, (t.k - 1) * (16 * G))
                    nc.vector.tensor_tensor(sidx[:, t.slot, :], move[:, t.slot, :], tiles(col["s"], t),
                                            ALU.add).then_inc(sidx4, 1)
                    equal_pairs(dve, t, "s", rows4, sums4, eq4)
                    dve.wait_ge(m_ps, t.k + 1)
                    if t.after(2):
                        dve.wait_ge(m4, t.k - 1)
                    nc.vector.tensor_tensor(pre[:, t.slot, :, :], bank[4 + t.slot][:, 0:P]
                                            .rearrange("p (t d) -> p t d", d=D),
                                            eb2r[:, :].unsqueeze(1).to_broadcast([P, G, D]), ALU.add).then_inc(pre4, 1)
                run_steps(dve, step)

            @block.tensor
            def _(pe):
                def step(t):
                    pe.wait_ge(he_in[t.load], t.load_turn * (32 * G))
                    if t.after(2):
                        pe.wait_ge(heT4, t.k - 1)
                    for j in range(G):
                        last = nc.tensor.transpose(bank[t.slot][:, j * P:(j + 1) * P], he[:, t.load, j, :], ident[:, :])
                    last.then_inc(heT_ps, 1)
                    pe.wait_ge(heT4, t.k + 1)
                    if t.after(2):
                        pe.wait_ge(hid4, t.k - 1)
                    nc.tensor.matmul(bank[2 + t.slot][:, 0:G * P], ew1[:, :], heT[:, t.slot, :],
                                     start=True, stop=True).then_inc(hid_ps, 1)
                    pe.wait_ge(hid4, t.k + 1)
                    if t.after(2):
                        pe.wait_ge(pre4, t.k - 1)
                    for j in range(G):
                        last = nc.tensor.matmul(bank[4 + t.slot][:, j * D:(j + 1) * D],
                                                hidE[:, t.slot, j * P:(j + 1) * P], ew2[:, :], start=True, stop=True)
                    last.then_inc(m_ps, 1)
                    pe.wait_ge(eq4, t.k + 1)
                    pe.wait_ge(m4, t.k + 1)
                    if t.after(2):
                        pe.wait_ge(v4, t.k - 1)
                    group_sums(t, bank[6 + t.slot], x1e[:, t.slot, :, :]).then_inc(sums4, 1)
                run_steps(pe, step)

        in5, y_out = ring("in5", DEEP), ring("y_out", 2)
        hmT_ps, hmT5, hn_ps, hn5 = ring("hmT_ps", 2), ring("hmT5", 2), ring("hn_ps", 2), ring("hn5", 2)
        (newton, on_ps, std5, res5, rs5, mean5, xc5, sq5, ss5, veps5, rstd5, fin5) = (
            sem(n) for n in ("newton", "on_ps", "std5", "res5", "rs5", "mean5", "xc5", "sq5", "ss5", "veps5", "rstd5",
                             "fin5"))

        def refine(dve, a, part):
            if not a.exists():
                return
            r = root[:, a.slot, :]
            if part == 0:
                dve.wait_ge(std5, a.k + 1)
                nc.vector.reciprocal(r, std[:, a.slot, :]).then_inc(newton, 1)
            elif part == 1:
                dve.wait_ge(newton, a.k * 3 + 1)
                nc.vector.tensor_tensor(square[:, a.slot, :], r, r, ALU.mult).then_inc(newton, 1)
            elif part == 2:
                dve.wait_ge(newton, a.k * 3 + 2)
                nc.vector.scalar_tensor_tensor(out=factor[:, a.slot, :], in0=square[:, a.slot, :], scalar=-0.5,
                                               in1=veps[:, a.load, :], op0=ALU.mult, op1=ALU.mult).then_inc(newton, 1)
            else:
                dve.wait_ge(newton, a.k * 3 + 3)
                if a.after(2):
                    dve.wait_ge(fin5, a.k - 1)
                nc.vector.scalar_tensor_tensor(out=rstd[:, a.slot, :], in0=factor[:, a.slot, :], scalar=1.5,
                                               in1=r, op0=ALU.add, op1=ALU.mult).then_inc(rstd5, 1)

        with nc.Block() as block:
            @block.sync
            def _(sp):
                def step(t):
                    a = t.plus(DEEP_LEAD)
                    if a.exists():
                        if a.after(DEEP):
                            sp.wait_ge(hmT_ps[1], a.k - DEEP + 1)
                            sp.wait_ge(res5, a.k - DEEP + 1)
                        sp.dma_start(hm[:, a.deep, :, 0, :], by_row(chunk_of(h, a))).then_inc(in5[a.deep], 16)
                        sp.dma_start(hm[:, a.deep, :, 1, :], by_row(chunk_of(msum, a))).then_inc(in5[a.deep], 16)
                    a = t.plus(-3)
                    if a.exists():
                        store_chunk(sp, a, out, fin5, y_out)
                run_steps(sp, step, before=DEEP_LEAD, after=3)
                for s in range(2):
                    sp.wait_ge(y_out[s], 16 * STEPS // 2)

            @block.tensor
            def _(pe):
                def step(t):
                    a = t.plus(1)
                    if a.exists():
                        pe.wait_ge(in5[a.deep], a.deep_turn * 32)
                        for half in range(2):
                            if a.after(1):
                                pe.wait_ge(hmT5[half], a.k)
                            for q in range(4):
                                r = 4 * half + q
                                last = nc.tensor.transpose(bank[half][:, q * P:(q + 1) * P],
                                                           hm[:, a.deep, r, :, :].rearrange("p m d -> p (m d)"), ident[:, :])
                            last.then_inc(hmT_ps[half], 1)
                    if t.exists():
                        for half in range(2):
                            pe.wait_ge(hmT5[half], t.k + 1)
                            if t.after(1):
                                pe.wait_ge(hn5[half], t.k)
                            nc.tensor.matmul(bank[2 + half][:, :], nw1[:, :],
                                             hmT[:, t.slot, half * 512:(half + 1) * 512],
                                             start=True, stop=True).then_inc(hn_ps[half], 1)
                    a = t.plus(-1)
                    if a.exists():
                        for half in range(2):
                            pe.wait_ge(hn5[half], a.k + 1)
                        if a.after(2):
                            pe.wait_ge(res5, a.k - 1)
                        nc.tensor.matmul(bank[4 + a.slot][:, :], ones[:, :], nb2parts[:, :],
                                         start=True, stop=False)
                        for r in range(ROWS):
                            last = nc.tensor.matmul(bank[4 + a.slot][:, r * D:(r + 1) * D],
                                                    hidN[:, a.slot, r * P:(r + 1) * P], nw2[:, :],
                                                    start=False, stop=(r == ROWS - 1))
                        last.then_inc(on_ps, 1)
                run_steps(pe, step, before=1, after=1)

            def spread(act, a, half):
                act.wait_ge(hmT_ps[half], a.k + 1)
                if a.after(2):
                    act.wait_ge(hn_ps[half], a.k - 1)
                nc.scalar.copy(hmT[:, a.slot, half * 512:(half + 1) * 512], bank[half][:, :]).then_inc(hmT5[half], 1)

            @block.scalar
            def _(act):
                def step(t):
                    a = t.plus(1)
                    if a.exists():
                        for half in range(2):
                            spread(act, a, half)
                    if t.exists():
                        for half in range(2):
                            act.wait_ge(hn_ps[half], t.k + 1)
                            if t.after(2):
                                act.wait_ge(on_ps, t.k - 1)
                            nc.scalar.activation(hidN[:, t.slot, half * 512:(half + 1) * 512], bank[2 + half][:, :],
                                                 ACT.Relu, bias=nb1c[:, 0:1]).then_inc(hn5[half], 1)
                    a = t.plus(-1)
                    if a.exists():
                        act.wait_ge(xc5, a.k + 1)
                        if a.after(2):
                            act.wait_ge(ss5, a.k - 1)
                        nc.scalar.activation(sq[:, a.slot, :], xc[:, a.load, :], ACT.Square).then_inc(sq5, 1)
                    a = t.plus(-2)
                    if a.exists():
                        act.wait_ge(veps5, a.k + 1)
                        if a.after(2):
                            act.wait_ge(rstd5, a.k - 1)
                        nc.scalar.activation(std[:, a.slot, :], veps[:, a.load, :], ACT.Sqrt).then_inc(std5, 1)
                run_steps(act, step, before=1, after=2)

            @block.vector
            def _(dve):
                def step(t):
                    a, b, c = t.plus(-1), t.plus(-2), t.plus(-3)
                    if a.exists():
                        dve.wait_ge(on_ps, a.k + 1)
                        if a.after(2):
                            dve.wait_ge(xc5, a.k - 1)
                        nc.vector.scalar_tensor_tensor(
                            out=by_row(res[:, a.slot, :]), in0=hm[:, a.deep, :, 0, :], scalar=2.0,
                            in1=by_row(bank[4 + a.slot][:, :]), op0=ALU.mult, op1=ALU.add).then_inc(res5, 1)
                    refine(dve, c, 0)
                    if a.exists():
                        row_sums(dve, a, res5, rs5)
                    refine(dve, c, 1)
                    if b.exists():
                        square_sums(dve, b, sq5, ss5)
                    if a.exists():
                        row_means(dve, a, rs5, mean5, xc5)
                    refine(dve, c, 2)
                    if b.exists():
                        row_variances(dve, b, ss5, veps5, rstd5)
                    refine(dve, c, 3)
                run_steps(dve, step, before=1, after=3)

            @block.gpsimd
            def _(pool):
                def step(t):
                    a = t.plus(-1)
                    if a.exists():
                        centre(pool, a, mean5, sq5, fin5, xc5)
                    a = t.plus(-3)
                    if a.exists():
                        scale_rows(pool, nc.gpsimd, a, rstd5, fin5, y_out)
                run_steps(pool, step, after=3)


_INS = ['x', 'src', 'dst', 'L0_gnn_W1', 'L0_gnn_b1', 'L0_gnn_W2', 'L0_gnn_b2', 'L1_gnn_eW1', 'L1_gnn_eb1',
        'L1_gnn_eW2', 'L1_gnn_eb2', 'L1_gnn_nW1', 'L1_gnn_nb1', 'L1_gnn_nW2', 'L1_gnn_nb2']


def kernel(**inputs):
    import numpy as _np
    import concourse.bacc as _bacc
    from concourse import mybir as _mybir
    from concourse.bass_utils import run_bass_kernel_spmd as _run

    nc = _bacc.Bacc("TRN2", target_bir_lowering=False, num_devices=1)
    arrays, args = {}, []
    for name in _INS:
        a = _np.ascontiguousarray(inputs[name])
        arrays[f"in_{name}_dram"] = a
        args.append(nc.dram_tensor(f"in_{name}_dram", a.shape, _mybir.dt.from_np(a.dtype), kind="ExternalInput").ap())
    args.append(nc.dram_tensor("out_0_dram", (100000, 64), _mybir.dt.float32, kind="ExternalOutput").ap())
    gnn_kernel(nc, *args)
    r = _run(nc, [arrays], core_ids=[0])
    return r.results[0]["out_0_dram"]
```

```python
import concourse.bass as bass
from concourse import mybir
from contextlib import ExitStack

N = 100000
D = 64
E = 25000
HID = 128
P = 128
TILES = -(-E // P)
LAST = E - (TILES - 1) * P
G = 2
STEPS = TILES // G
ROWS = 8
CHUNK = P * ROWS
TABLE = STEPS * CHUNK
PAD_ROW = N + P
LN_EPS = 1e-5
ACT_ROWS = 6
ZCOLS = 56 * D
ZDMAS = TABLE * D // (P * ZCOLS)
assert STEPS == -(-N // CHUNK) and TILES % G == 0 and TABLE >= N + G * P
assert ZDMAS * P * ZCOLS == TABLE * D and ZDMAS % 2 == 0

UNROLL = 8
HEAD, TAIL = 8, 88
DEEP = 8
LEAD = 6
GATHER_LEAD = 4
ADD_LAG = 2
FOUR = 4


class At:

    def __init__(self, i, c):
        self.i, self.c, self.fixed = i, c, isinstance(i, int)
        self.slot = c % 2
        self.four = c % FOUR
        self.deep = c % DEEP

    def plus(self, d):
        return At(self.i, self.c + d)

    @property
    def k(self):
        return self.i * UNROLL + self.c

    @property
    def turn(self):
        return self.i * (UNROLL // 2) + (self.c // 2 + 1)

    @property
    def deep_turn(self):
        return self.i * (UNROLL // DEEP) + (self.c // DEEP + 1)

    def exists(self):
        return not self.fixed or 0 <= self.c < STEPS

    def after(self, n):
        return not self.fixed or self.c >= n

    def last(self):
        return self.fixed and self.c == STEPS - 1

    def start(self):
        return N - CHUNK if self.last() else self.k * CHUNK


def run_steps(eng, step, before=0, after=0):
    for t in range(-before, HEAD):
        step(At(0, t))
    with eng.Fori(HEAD // UNROLL, TAIL // UNROLL) as i:
        for c in range(UNROLL):
            step(At(i, c))
    for t in range(TAIL, STEPS + after):
        step(At(0, t))


def gnn_kernel(nc, x, src, dst, W1, b1, W2, b2, eW1, eb1, eW2, eb2, nW1, nb1, nW2, nb2, out):
    f32, i32, bf16 = mybir.dt.float32, mybir.dt.int32, mybir.dt.bfloat16
    ALU = mybir.AluOpType
    ACT = mybir.ActivationFunctionType
    AX = mybir.AxisListType.X

    with ExitStack() as ctx:
        def sb(name, shape, dt=f32):
            return ctx.enter_context(nc.sbuf_tensor(name, shape, dt))

        def sem(name):
            return ctx.enter_context(nc.semaphore(name))

        def ring(name, slots):
            return [sem(f"{name}_{s}") for s in range(slots)]

        ctx.enter_context(nc.allow_non_contiguous_dma(reason="bias columns, once"))

        def dram(name, shape, dt=f32):
            return nc.dram_tensor(name, shape, dt, kind="Internal").ap()

        agg0 = dram("agg0", [TABLE, D])
        agg1 = dram("agg1", [TABLE, D])
        msum = dram("msum", [TABLE, D])
        x1T = dram("x1T", [STEPS, P, 512])
        hT = dram("hT", [STEPS, P, 512])
        h = dram("h", [N, D])
        rows_src = dram("rows_src", [TILES, P], i32)
        rows_dst = dram("rows_dst", [TILES, P], i32)

        ident = sb("ident", [P, P])
        before = sb("before", [P, G, G * P])
        zeros = sb("zeros", [P, ZCOLS])
        mhalf = sb("mhalf", [P, ROWS])
        w1bd = [sb(f"w1bd{l}", [P, P]) for l in range(2)]
        w2bd = [sb(f"w2bd{l}", [P, P]) for l in range(2)]
        b1c = sb("b1c", [P, 2])
        b2c = sb("b2c", [P, 1])
        b2r = sb("b2r", [P, D])
        ones = sb("ones", [P, P], bf16)
        b2parts = sb("b2parts", [P, 512], bf16)
        taken = sb("taken", [1, 3, D])
        rest = sb("rest", [1, 3, D])
        b2row = sb("b2row", [1, D])
        nb2r = sb("nb2r", [P, D])
        ew1, ew2 = sb("ew1", [2 * D, HID]), sb("ew2", [HID, D])
        nw1, nw2 = sb("nw1", [2 * D, HID]), sb("nw2", [HID, D])
        nw1s = sb("nw1s", [2 * D, HID])
        eb1c, nb1c = sb("eb1c", [HID, 1]), sb("nb1c", [HID, 1])
        eb2r = sb("eb2r", [P, D])

        idx_rows = {n: sb(f"idx_rows_{n}", [P, 2, P], i32) for n in "sd"}
        idx_rowf = {n: sb(f"idx_rowf_{n}", [P, 2, P]) for n in "sd"}
        col = {n: sb(f"col_{n}", [P, TILES]) for n in "sd"}
        gat = {n: sb(f"gat_{n}", [P, TILES], i32) for n in "sd"}
        away = {n: sb(f"away_{n}", [P, TILES]) for n in "sd"}
        scat_d = sb("scat_d", [P, TILES], i32)
        diff = sb("diff", [P, P], i32)
        sparei = sb("sparei", [P, G], i32)
        spare = sb("spare", [P, G])

        rowbc = sb("rowbc", [P, 2, G * P], i32)
        eq = sb("eq", [P, 2, G, G * P])
        seen = sb("seen", [P, G, G * P])
        cnt = sb("cnt", [P, 2, G])
        move = sb("move", [P, 2, G])
        gidx = sb("gidx", [P, DEEP, 2, G], i32)
        sidx = sb("sidx", [P, FOUR, G], i32)
        xs_ring = sb("xs_ring", [P, DEEP, G, D])
        xs_all = sb("xs_all", [P, TILES, D])
        ye = sb("ye", [P, 2, G, D])
        yeT = sb("yeT", [P, 2, P])
        hidE = sb("hidE", [P, 2, G * P])
        x1e = sb("x1e", [P, 2, G, D])
        pre = sb("pre", [P, 2, G, D])
        vout = sb("vout", [P, FOUR, G, D])
        he = sb("he", [P, DEEP, G, 2 * D])
        heT = sb("heT", [P, 2, G * P])

        xin = sb("xin", [P, DEEP, 512])
        ain = sb("ain", [P, DEEP, 512])
        yd = sb("yd", [P, 2, 512])
        ydT = sb("ydT", [P, 2, 512])
        hd = sb("hd", [P, 2, 512])
        x1o = sb("x1o", [P, 2, 512])
        base = sb("base", [P, 2, 512])
        res = sb("res", [P, 2, 512])
        xc = sb("xc", [P, FOUR, 512])
        sq = sb("sq", [P, 2, 512])
        fin = sb("fin", [P, 2, 512])
        room = xs_all[:, :, :].rearrange("p t d -> p (t d)")
        xin3, ain3, tin3 = (room[:, n * DEEP * 512:(n + 1) * DEEP * 512].rearrange("p (s n) -> p s n", s=DEEP)
                            for n in range(3))
        hmT = room[:, 0:DEEP * 1024].rearrange("p (s n) -> p s n", s=DEEP)
        hidN = sb("hidN", [P, 2, 1024])
        mean = sb("mean", [P, 2, ROWS])
        rsum = sb("rsum", [P, 2, ROWS])
        ssum = sb("ssum", [P, 2, ROWS])
        veps = sb("veps", [P, FOUR, ROWS])
        std, root, square, factor = (sb(n, [P, 2, ROWS]) for n in ("std", "root", "square", "factor"))
        rstd = sb("rstd", [P, 2, ROWS])

        bank = [ctx.enter_context(nc.psum_tensor(f"bank{i}", [P, 512], f32)) for i in range(8)]

        def chunk_of(table, at):
            return table[bass.ds(at.start(), CHUNK), :].rearrange("(p r) d -> p (r d)", p=P)

        def group_rows(rows, at):
            return rows[bass.ds(at.k * G, G), :].rearrange("t e -> (t e)").partition_broadcast(P)

        def tiles(table, at):
            return table[:, bass.ds(at.k * G, G)]

        def zero_pieces(eng, first, end):
            flat = agg0.rearrange("(z p r) d -> z p (r d)", z=ZDMAS, p=P)
            for z in range(first, end):
                if z >= 2:
                    eng.wait_ge(zeroed0[z % 2], 16 * (z // 2))
                eng.dma_start(flat[z, :, :], zeros[:, :]).then_inc(zeroed0[z % 2], 16)

        turns = sem("turns")
        zeroed0, cleared = ring("zeroed0", 2), sem("cleared")

        idx_in, rows_out, w_clear, w_in = (sem(n) for n in ("idx_in", "rows_out", "w_clear", "w_in"))
        iotas, consts, idx_f, idx_T, tab, zeros_made, parts, took = (
            sem(n) for n in ("iotas", "consts", "idx_f", "idx_T", "tab", "zeros_made", "parts", "took"))
        W_DMAS = 26
        lists = {"s": (src, rows_src), "d": (dst, rows_dst)}
        full = (TILES - 1 - P) * P

        with nc.Block() as block:
            @block.gpsimd
            def _(pool):
                for n in "sd":
                    nc.gpsimd.iota(idx_rows[n][:, 1, :], pattern=[[1, P]], base=PAD_ROW,
                                   channel_multiplier=0).then_inc(iotas, 1)
                nc.gpsimd.iota(diff[:, :], pattern=[[1, P]], base=0, channel_multiplier=-1).then_inc(iotas, 1)
                nc.gpsimd.iota(sparei[:, :], pattern=[[P, G]], base=N, channel_multiplier=1).then_inc(iotas, 1)

            @block.sync
            def _(sp):
                sp.wait_ge(iotas, 2)
                for n in "sd":
                    lst = lists[n][0]
                    sp.dma_start(idx_rows[n][:, 0, :],
                                 lst[0:P * P].rearrange("(t e) -> t e", e=P)).then_inc(idx_in, 16)
                    sp.dma_start(idx_rows[n][0:TILES - 1 - P, 1, :],
                                 lst[P * P:P * P + full].rearrange("(t e) -> t e", e=P)).then_inc(idx_in, 16)
                    sp.dma_start(idx_rows[n][TILES - 1 - P:TILES - P, 1, 0:LAST],
                                 lst[E - LAST:E].rearrange("(t e) -> t e", e=LAST)).then_inc(idx_in, 16)
                sp.wait_ge(w_clear, 4)
                for l in range(2):
                    for q in range(2):
                        a = slice(q * D, (q + 1) * D)
                        sp.dma_start(w1bd[l][a, a], W1[l, :, :]).then_inc(w_in, 16)
                        sp.dma_start(w2bd[l][a, a], W2[l, :, :]).then_inc(w_in, 16)
                        sp.dma_start(b1c[a, l:l + 1], b1[l, :].rearrange("(d o) -> d o", o=1)).then_inc(w_in, 16)
                for q in range(2):
                    sp.dma_start(b2c[q * D:(q + 1) * D, :],
                                 b2[0, :].rearrange("(d o) -> d o", o=1)).then_inc(w_in, 16)
                for to, of in ((ew1, eW1), (ew2, eW2), (nw1, nW1), (nw2, nW2)):
                    sp.dma_start(to[:, :], of).then_inc(w_in, 16)
                for q in range(2):
                    sp.dma_start(nw1s[q * D:(q + 1) * D, :], nW1[(1 - q) * D:(2 - q) * D, :]).then_inc(w_in, 16)
                for to, of in ((eb1c, eb1), (nb1c, nb1)):
                    sp.dma_start(to[:, :], of.rearrange("(d o) -> d o", o=1)).then_inc(w_in, 16)
                for to, of in ((eb2r, eb2), (b2r, b2[0, :]), (nb2r, nb2)):
                    sp.dma_start(to[:, :], of.partition_broadcast(P)).then_inc(w_in, 16)
                sp.dma_start(b2row[:, :], b2[1:2, :]).then_inc(w_in, 16)
                sp.wait_ge(idx_in, 96)
                for n in "sd":
                    rows = lists[n][1]
                    sp.dma_start(rows[0:P, :], idx_rows[n][:, 0, :]).then_inc(rows_out, 16)
                    sp.dma_start(rows[P:TILES, :], idx_rows[n][0:TILES - P, 1, :]).then_inc(rows_out, 16)
                sp.wait_ge(rows_out, 64)
                sp.wait_ge(w_in, 16 * W_DMAS)

            @block.scalar
            def _(act):
                act.wait_ge(zeros_made, 1)
                zero_pieces(act, 0, ZDMAS // 2)

            @block.vector
            def _(dve):
                nc.vector.memset(zeros[:, :], 0.0).then_inc(zeros_made, 1)
                for w in (*w1bd, *w2bd):
                    nc.vector.memset(w[:, :], 0.0).then_inc(w_clear, 1)
                nc.vector.memset(mhalf[:, :], -0.5)
                nc.vector.memset(ones[:, :], 1.0)
                nc.vector.memset(b2parts[:, :], 0.0).then_inc(parts, 1)
                nc.vector.memset(before[:, 0, P:2 * P], 0.0)
                nc.vector.memset(before[:, 1, 0:P], 1.0)
                dve.wait_ge(iotas, 4)
                nc.vector.tensor_scalar(ident[:, :], diff[:, :], 0.0, None, ALU.is_equal).then_inc(consts, 1)
                nc.vector.tensor_scalar(before[:, 0, 0:P], diff[:, :], 0.0, None, ALU.is_lt)
                nc.vector.tensor_scalar(before[:, 1, P:2 * P], diff[:, :], 0.0, None, ALU.is_lt)
                nc.vector.tensor_copy(spare[:, :], sparei[:, :]).then_inc(tab, 1)
                dve.wait_ge(idx_in, 96)
                for n in "sd":
                    nc.vector.tensor_copy(idx_rowf[n][:, :, :], idx_rows[n][:, :, :]).then_inc(idx_f, 1)
                for m, n in enumerate("sd"):
                    dve.wait_ge(idx_T, m + 1)
                    nc.vector.tensor_copy(col[n][:, 0:P], bank[2 * m][:, 0:P])
                    nc.vector.tensor_copy(col[n][:, P:TILES], bank[2 * m + 1][:, 0:TILES - P]).then_inc(tab, 1)
                    dve.wait_ge(tab, m + 2)
                    nc.vector.tensor_scalar(gat[n][:, :], col[n][:, :], float(N - 1), None, ALU.min)
                    nc.vector.tensor_tensor(away[n][:, :].rearrange("p (g t) -> p g t", t=G),
                                            spare[:, :].unsqueeze(1).to_broadcast([P, STEPS, G]),
                                            col[n][:, :].rearrange("p (g t) -> p g t", t=G), ALU.subtract)

                dve.wait_ge(w_in, 16 * W_DMAS)
                for part in range(3):
                    of = b2row[:, :] if part == 0 else rest[:, part - 1, :]
                    dve.wait_ge(parts, 1 + 2 * part)
                    nc.vector.tensor_copy(b2parts[32 * part:32 * part + 1, :].rearrange("o (r d) -> o r d", d=D),
                                          of.unsqueeze(1).to_broadcast([1, ROWS, D])).then_inc(parts, 1)
                    dve.wait_ge(parts, 2 + 2 * part)
                    nc.vector.tensor_copy(taken[:, part, :], b2parts[32 * part:32 * part + 1, 0:D]).then_inc(took, 1)
                    dve.wait_ge(took, part + 1)
                    nc.vector.tensor_tensor(rest[:, part, :], of, taken[:, part, :], ALU.subtract).then_inc(parts, 1)

            @block.tensor
            def _(pe):
                pe.wait_ge(consts, 1)
                for m, n in enumerate("sd"):
                    pe.wait_ge(idx_f, m + 1)
                    for part in range(2):
                        last = nc.tensor.transpose(bank[2 * m + part][:, 0:P], idx_rowf[n][:, part, :], ident[:, :])
                    last.then_inc(idx_T, 1)

        def equal_pairs(dve, at, n, sums_done, eq_ready):
            if at.after(2):
                dve.wait_ge(sums_done, at.k - 1)
            for t in range(G):
                last = nc.vector.tensor_scalar(eq[:, at.slot, t, :], rowbc[:, at.slot, :],
                                               col[n][:, bass.ds(at.k * G + t, 1)], None, ALU.is_equal)
            last.then_inc(eq_ready, 1)

        def scatter_rows(dve, at, n, cnt_done, move_done):
            for t in range(G):
                last = nc.vector.scalar_tensor_tensor(
                    out=seen[:, t, :], in0=rowbc[:, at.slot, :], scalar=col[n][:, bass.ds(at.k * G + t, 1)],
                    in1=before[:, t, :], op0=ALU.is_equal, op1=ALU.mult, accum_out=cnt[:, at.slot, t:t + 1])
            last.then_inc(cnt_done, 1)
            dve.wait_ge(cnt_done, at.k + 1)
            nc.vector.scalar_tensor_tensor(out=move[:, at.slot, :], in0=cnt[:, at.slot, :], scalar=1.0,
                                           in1=tiles(away[n], at), op0=ALU.min, op1=ALU.mult).then_inc(move_done, 1)
            dve.wait_ge(move_done, at.k + 1)

        def group_sums(at, psum, values):
            for j in range(G):
                for t in range(G):
                    last = nc.tensor.matmul(psum[:, j * D:(j + 1) * D], eq[:, at.slot, t, j * P:(j + 1) * P],
                                            values[:, t, :], start=(t == 0), stop=(t == G - 1))
            return last

        def add_group(pool, at, table, v_ready, rows_ready, added, zeroed):
            if at.fixed and at.c == 0:
                for semaphore, count in zeroed:
                    pool.wait_ge(semaphore, count)
            pool.wait_ge(v_ready, at.k + 1)
            pool.wait_ge(rows_ready, at.k + 1)
            if at.after(1):
                pool.wait_ge(added, at.k * (16 * G))
            carry_waits(pool)
            for t in range(G):
                nc.gpsimd.indirect_dma_start(
                    table, bass.IndirectOffsetOnAxis(ap=sidx[:, at.four, t:t + 1], axis=0),
                    vout[:, at.four, t, :], None, compute_op=ALU.add).then_inc(added, 16)

        def carry_waits(pool):
            pool.sem_inc(turns, 1)

        def gather_group(pool, at, table, to, list_slot, landed):
            carry_waits(pool)
            for t in range(G):
                nc.gpsimd.indirect_dma_start(
                    to[:, t, :], None, table,
                    bass.IndirectOffsetOnAxis(ap=gidx[:, at.deep, list_slot, t:t + 1], axis=0)).then_inc(landed, 16)

        rows_in, xs_in = ring("rows", 2), ring("xs_in", DEEP)
        gidx1, xs_kept, eq1, cnt1, move1, sidx1, sums1, v1, added0 = (
            sem(n) for n in ("gidx1", "xs_kept", "eq1", "cnt1", "move1", "sidx1", "sums1", "v1", "added0"))

        with nc.Block() as block:
            @block.sync
            def _(sp):
                def step(t):
                    a = t.plus(2)
                    if a.exists():
                        if a.after(2):
                            sp.wait_ge(eq1, a.k - 1)
                        sp.dma_start(rowbc[:, a.slot, :], group_rows(rows_dst, a)).then_inc(rows_in[a.slot], 16)
                    if t.exists():
                        if t.fixed and t.c == 0:
                            zero_pieces(sp, ZDMAS // 2, ZDMAS)
                            for z in zeroed0:
                                sp.wait_ge(z, 8 * ZDMAS)
                        for table in (agg1, msum):
                            sp.dma_start(table[bass.ds(t.k * CHUNK, CHUNK), :].rearrange("(p r) d -> p (r d)", p=P),
                                         zeros[:, 0:512]).then_inc(cleared, 16)
                run_steps(sp, step, before=2)

            @block.gpsimd
            def _(pool):
                def step(t):
                    a = t.plus(GATHER_LEAD)
                    if a.exists():
                        pool.wait_ge(gidx1, a.k + 1)
                        if a.after(DEEP):
                            pool.wait_ge(xs_kept, a.k - DEEP + 1)
                            pool.wait_ge(sums1, a.k - DEEP + 1)
                        gather_group(pool, a, x, xs_ring[:, a.deep, :, :], 0, xs_in[a.deep])
                    a = t.plus(-1)
                    if a.exists():
                        add_group(pool, a, agg0, v1, sidx1, added0, [(z, 8 * ZDMAS) for z in zeroed0])
                run_steps(pool, step, before=GATHER_LEAD, after=1)
                pool.wait_ge(added0, 16 * TILES)

            @block.scalar
            def _(act):
                def step(t):
                    a = t.plus(GATHER_LEAD)
                    if a.exists():
                        nc.scalar.copy(gidx[:, a.deep, 0, :], tiles(gat["s"], a)).then_inc(gidx1, 1)
                    if t.exists():
                        act.wait_ge(xs_in[t.deep], t.deep_turn * (16 * G))
                        nc.scalar.copy(xs_all[:, bass.ds(t.k * G, G), :], xs_ring[:, t.deep, :, :]).then_inc(xs_kept, 1)
                        act.wait_ge(sums1, t.k + 1)
                        if t.after(FOUR):
                            act.wait_ge(added0, (t.k - FOUR + 1) * (16 * G))
                        nc.scalar.copy(vout[:, t.four, :, :], bank[t.slot][:, 0:P]
                                       .rearrange("p (t d) -> p t d", d=D)).then_inc(v1, 1)
                run_steps(act, step, before=GATHER_LEAD)

            @block.vector
            def _(dve):
                def step(t):
                    dve.wait_ge(rows_in[t.slot], t.turn * 16)
                    scatter_rows(dve, t, "d", cnt1, move1)
                    nc.vector.tensor_tensor(tiles(scat_d, t), move[:, t.slot, :], tiles(col["d"], t), ALU.add)
                    if t.after(FOUR):
                        dve.wait_ge(added0, (t.k - FOUR + 1) * (16 * G))
                    nc.vector.tensor_tensor(sidx[:, t.four, :], move[:, t.slot, :], tiles(col["d"], t),
                                            ALU.add).then_inc(sidx1, 1)
                    equal_pairs(dve, t, "d", sums1, eq1)
                run_steps(dve, step)

            @block.tensor
            def _(pe):
                def step(t):
                    pe.wait_ge(eq1, t.k + 1)
                    pe.wait_ge(xs_in[t.deep], t.deep_turn * (16 * G))
                    if t.after(2):
                        pe.wait_ge(v1, t.k - 1)
                    group_sums(t, bank[t.slot], xs_ring[:, t.deep, :, :]).then_inc(sums1, 1)
                run_steps(pe, step)

        x1_out, ag_in, xd_in = ring("x1_out", 2), ring("ag_in", DEEP), ring("xd_in", DEEP)
        (gidx2, sidx2, ye2, yeT_ps, yeT2, hide_ps, hide2, x1e_ps, x1e2, eq2, sums2, v2, added1,
         yd2, ydT_ps, ydT2, hd_ps, hd2, x1_ps, x1_made) = (
            sem(n) for n in ("gidx2", "sidx2", "ye2", "yeT_ps", "yeT2", "hide_ps", "hide2", "x1e_ps", "x1e2",
                             "eq2", "sums2", "v2", "added1", "yd2", "ydT_ps", "ydT2", "hd_ps", "hd2",
                             "x1_ps", "x1_made"))

        with nc.Block() as block:
            @block.sync
            def _(sp):
                def step(t):
                    a = t.plus(1)
                    if a.exists():
                        if a.after(2):
                            sp.wait_ge(eq2, a.k - 1)
                        sp.dma_start(rowbc[:, a.slot, :], group_rows(rows_dst, a)).then_inc(rows_in[a.slot], 16)
                    a = t.plus(-1)
                    if a.exists():
                        sp.wait_ge(x1_made, a.k + 1)
                        sp.dma_start(x1T[bass.ds(a.k, 1), :, :].rearrange("o p n -> (o p) n"),
                                     x1o[:, a.slot, :]).then_inc(x1_out[a.slot], 16)
                    a = t.plus(LEAD)
                    if a.exists():
                        if a.after(DEEP):
                            sp.wait_ge(yd2, a.k - DEEP + 1)
                        sp.dma_start(xin[:, a.deep, :], chunk_of(x, a)).then_inc(xd_in[a.deep], 16)
                        sp.dma_start(ain[:, a.deep, :], chunk_of(agg0, a)).then_inc(xd_in[a.deep], 16)
                run_steps(sp, step, before=LEAD, after=1)
                for s in range(2):
                    sp.wait_ge(x1_out[s], 16 * STEPS // 2)

            @block.gpsimd
            def _(pool):
                def step(t):
                    a = t.plus(GATHER_LEAD)
                    if a.exists():
                        pool.wait_ge(gidx2, a.k + 1)
                        if a.after(DEEP):
                            pool.wait_ge(ye2, a.k - DEEP + 1)
                        gather_group(pool, a, agg0, xs_ring[:, a.deep, :, :], 0, ag_in[a.deep])
                    a = t.plus(-ADD_LAG)
                    if a.exists():
                        add_group(pool, a, agg1, v2, sidx2, added1, [(cleared, 32 * STEPS)])
                run_steps(pool, step, before=GATHER_LEAD, after=ADD_LAG)
                pool.wait_ge(added1, 16 * TILES)

            @block.scalar
            def _(act):
                def step(t):
                    a = t.plus(GATHER_LEAD)
                    if a.exists():
                        if a.after(DEEP):
                            act.wait_ge(ag_in[a.deep], (a.deep_turn - 1) * (16 * G))
                        nc.scalar.copy(gidx[:, a.deep, 0, :], tiles(gat["s"], a)).then_inc(gidx2, 1)
                    if t.exists():
                        act.wait_ge(hide_ps, t.k + 1)
                        if t.after(2):
                            act.wait_ge(x1e_ps, t.k - 1)
                        nc.scalar.activation(hidE[:, t.slot, 0:P], bank[1][:, 0:P], ACT.Tanh,
                                             bias=b1c[:, 0:1]).then_inc(hide2, 1)
                        act.wait_ge(hd_ps, t.k + 1)
                        if t.after(2):
                            act.wait_ge(x1_ps, t.k - 1)
                        nc.scalar.activation(hd[:, t.slot, :], bank[5][:, :], ACT.Tanh,
                                             bias=b1c[:, 0:1]).then_inc(hd2, 1)
                    a = t.plus(-2)
                    if a.exists():
                        if a.after(FOUR):
                            act.wait_ge(added1, (a.k - FOUR + 1) * (16 * G))
                        nc.scalar.copy(sidx[:, a.four, :], tiles(scat_d, a)).then_inc(sidx2, 1)
                        act.wait_ge(sums2, a.k + 1)
                        nc.scalar.copy(vout[:, a.four, :, :], bank[3][:, 0:P]
                                       .rearrange("p (t d) -> p t d", d=D)).then_inc(v2, 1)
                    a = t.plus(-1)
                    if a.exists():
                        act.wait_ge(x1_ps, a.k + 1)
                        if a.after(2):
                            act.wait_ge(x1_out[a.slot], (a.turn - 1) * 16)
                        nc.scalar.activation(x1o[:, a.slot, :], bank[6][:, :], ACT.Identity,
                                             bias=b2c[:, 0:1]).then_inc(x1_made, 1)
                run_steps(act, step, before=GATHER_LEAD, after=2)

            @block.vector
            def _(dve):
                def step(t):
                    a = t.plus(1)
                    if a.exists():
                        dve.wait_ge(yeT_ps, a.k + 1)
                        if a.after(2):
                            dve.wait_ge(hide_ps, a.k - 1)
                        nc.vector.tensor_copy(yeT[:, a.slot, :], bank[0][:, 0:P]).then_inc(yeT2, 1)
                    b = t.plus(-1)
                    if b.exists():
                        dve.wait_ge(x1e_ps, b.k + 1)
                        if b.after(2):
                            dve.wait_ge(sums2, b.k - 1)
                        nc.vector.tensor_tensor(x1e[:, b.slot, :, :], bank[2][:, 0:P]
                                                .rearrange("p (t d) -> p t d", d=D),
                                                b2r[:, :].unsqueeze(1).to_broadcast([P, G, D]), ALU.add).then_inc(x1e2, 1)
                    if a.exists():
                        dve.wait_ge(ydT_ps, a.k + 1)
                        if a.after(2):
                            dve.wait_ge(hd_ps, a.k - 1)
                        nc.vector.tensor_copy(ydT[:, a.slot, :], bank[4][:, :]).then_inc(ydT2, 1)
                    a = t.plus(2)
                    if a.exists():
                        dve.wait_ge(ag_in[a.deep], a.deep_turn * (16 * G))
                        if a.after(2):
                            dve.wait_ge(yeT_ps, a.k - 1)
                        nc.vector.tensor_tensor(ye[:, a.slot, :, :], xs_all[:, bass.ds(a.k * G, G), :],
                                                xs_ring[:, a.deep, :, :], ALU.add).then_inc(ye2, 1)
                        dve.wait_ge(xd_in[a.deep], a.deep_turn * 32)
                        if a.after(2):
                            dve.wait_ge(ydT_ps, a.k - 1)
                        nc.vector.tensor_tensor(yd[:, a.slot, :], xin[:, a.deep, :], ain[:, a.deep, :],
                                                ALU.add).then_inc(yd2, 1)
                    if b.exists():
                        dve.wait_ge(rows_in[b.slot], (STEPS // 2 + b.turn) * 16)
                        equal_pairs(dve, b, "d", sums2, eq2)
                run_steps(dve, step, before=2, after=1)

            @block.tensor
            def _(pe):
                def step(t):
                    n, b = t.plus(1), t.plus(-1)
                    if n.exists():
                        pe.wait_ge(ye2, n.k + 1)
                        if n.after(1):
                            pe.wait_ge(yeT2, n.k)
                        nc.tensor.transpose(bank[0][:, 0:P], ye[:, n.slot, :, :].rearrange("p t d -> p (t d)"),
                                            ident[:, :]).then_inc(yeT_ps, 1)
                    if b.exists():
                        pe.wait_ge(hide2, b.k + 1)
                        if b.after(1):
                            pe.wait_ge(x1e2, b.k)
                        nc.tensor.matmul(bank[2][:, 0:P], hidE[:, b.slot, 0:P], w2bd[0][:, :],
                                         start=True, stop=True).then_inc(x1e_ps, 1)
                    if n.exists():
                        pe.wait_ge(yd2, n.k + 1)
                        if n.after(1):
                            pe.wait_ge(ydT2, n.k)
                        for q in range(4):
                            last = nc.tensor.transpose(bank[4][:, q * P:(q + 1) * P],
                                                       yd[:, n.slot, q * P:(q + 1) * P], ident[:, :])
                        last.then_inc(ydT_ps, 1)
                    if t.exists():
                        pe.wait_ge(yeT2, t.k + 1)
                        if t.after(1):
                            pe.wait_ge(hide2, t.k)
                        nc.tensor.matmul(bank[1][:, 0:P], w1bd[0][:, :], yeT[:, t.slot, :],
                                         start=True, stop=True).then_inc(hide_ps, 1)
                        pe.wait_ge(ydT2, t.k + 1)
                        if t.after(1):
                            pe.wait_ge(hd2, t.k)
                        nc.tensor.matmul(bank[5][:, :], w1bd[0][:, :], ydT[:, t.slot, :],
                                         start=True, stop=True).then_inc(hd_ps, 1)
                    a = t.plus(-2)
                    if a.exists():
                        pe.wait_ge(eq2, a.k + 1)
                        pe.wait_ge(x1e2, a.k + 1)
                        if a.after(1):
                            pe.wait_ge(v2, a.k)
                        group_sums(a, bank[3], x1e[:, a.slot, :, :]).then_inc(sums2, 1)
                    if b.exists():
                        pe.wait_ge(hd2, b.k + 1)
                        if b.after(1):
                            pe.wait_ge(x1_made, b.k)
                        nc.tensor.matmul(bank[6][:, :], w2bd[0][:, :], hd[:, b.slot, :],
                                         start=True, stop=True).then_inc(x1_ps, 1)
                run_steps(pe, step, before=1, after=2)

        in3, h_out = ring("in3", DEEP), ring("h_out", 2)
        (z_ps, z3, hz_ps, hz3, o_ps, res3, rs3, mean3, xc3, sq3, ss3, veps3, rstd3, fin3, rest3) = (
            sem(n) for n in ("z_ps", "z3", "hz_ps", "hz3", "o_ps", "res3", "rs3", "mean3", "xc3", "sq3",
                             "ss3", "veps3", "rstd3", "fin3", "rest3"))

        def by_row(t):
            return t.rearrange("p (r d) -> p r d", d=D)

        def wide(t):
            return t.unsqueeze(2).to_broadcast([P, ROWS, D])

        def row_sums(dve, a, res_done, rsum_done):
            dve.wait_ge(res_done, a.k + 1)
            nc.vector.tensor_reduce(rsum[:, a.slot, :], by_row(res[:, a.slot, :]), AX, ALU.add).then_inc(rsum_done, 1)

        def row_means(dve, a, rsum_done, mean_done, xc_done):
            dve.wait_ge(rsum_done, a.k + 1)
            if a.after(2):
                dve.wait_ge(xc_done, a.k - 1)
            nc.vector.tensor_scalar(mean[:, a.slot, :], rsum[:, a.slot, :], 1.0 / D, None,
                                    ALU.mult).then_inc(mean_done, 1)

        def square_sums(dve, a, sq_done, ss_done):
            dve.wait_ge(sq_done, a.k + 1)
            nc.vector.tensor_reduce(ssum[:, a.slot, :], by_row(sq[:, a.slot, :]), AX, ALU.add).then_inc(ss_done, 1)

        def row_variances(dve, a, ss_done, veps_done, rstd_done):
            dve.wait_ge(ss_done, a.k + 1)
            if a.after(FOUR):
                dve.wait_ge(rstd_done, a.k - 3)
            nc.vector.tensor_scalar(veps[:, a.four, :], ssum[:, a.slot, :], 1.0 / D, LN_EPS,
                                    ALU.mult, ALU.add).then_inc(veps_done, 1)

        def centre(pool, a, mean_done, sq_done, fin_done, xc_done):
            pool.wait_ge(mean_done, a.k + 1)
            if a.after(FOUR):
                for done in fin_done:
                    pool.wait_ge(done, a.k - 3)
                pool.wait_ge(sq_done, a.k - 3)
            nc.gpsimd.tensor_tensor(by_row(xc[:, a.four, :]), by_row(res[:, a.slot, :]),
                                    wide(mean[:, a.slot, :]), ALU.subtract).then_inc(xc_done, 1)

        def store_chunk(sp, a, table, fin_done, stored):
            for done in fin_done:
                sp.wait_ge(done, a.k + 1)
            if a.last():
                sp.wait_ge(stored[1 - a.slot], 16 * (STEPS // 2))
            sp.dma_start(chunk_of(table, a), fin[:, a.slot, :]).then_inc(stored[a.slot], 16)

        with nc.Block() as block:
            @block.sync
            def _(sp):
                def step(t):
                    a = t.plus(LEAD)
                    if a.exists():
                        if a.after(DEEP):
                            sp.wait_ge(z3, a.k - DEEP + 1)
                            sp.wait_ge(res3, a.k - DEEP + 1)
                        sp.dma_start(ain3[:, a.deep, :], chunk_of(agg1, a)).then_inc(in3[a.deep], 16)
                        sp.dma_start(tin3[:, a.deep, :], x1T[bass.ds(a.k, 1), :, :]
                                     .rearrange("o p n -> (o p) n")).then_inc(in3[a.deep], 16)
                        sp.dma_start(xin3[:, a.deep, :], chunk_of(x, a)).then_inc(in3[a.deep], 16)
                    a = t.plus(-3)
                    if a.exists():
                        store_chunk(sp, a, h, (fin3, rest3), h_out)
                run_steps(sp, step, before=LEAD, after=3)
                for s in range(2):
                    sp.wait_ge(h_out[s], 16 * STEPS // 2)

            @block.tensor
            def _(pe):
                def step(t):
                    a = t.plus(-1)
                    if a.exists():
                        pe.wait_ge(hz3, a.k + 1)
                        if a.after(2):
                            pe.wait_ge(res3, a.k - 1)
                        nc.tensor.matmul(bank[4 + a.slot][:, :], ones[:, :], b2parts[:, :],
                                         start=True, stop=False)
                        for q in range(4):
                            last = nc.tensor.matmul(bank[4 + a.slot][:, q * P:(q + 1) * P],
                                                    hd[:, a.slot, q * P:(q + 1) * P], w2bd[1][:, :],
                                                    start=False, stop=(q == 3))
                        last.then_inc(o_ps, 1)
                    if t.exists():
                        pe.wait_ge(z3, t.k + 1)
                        if t.after(2):
                            pe.wait_ge(hz3, t.k - 1)
                        nc.tensor.matmul(bank[2 + t.slot][:, :], w1bd[1][:, :], ydT[:, t.slot, :],
                                         start=True, stop=True).then_inc(hz_ps, 1)
                    a = t.plus(2)
                    if a.exists():
                        pe.wait_ge(in3[a.deep], a.deep_turn * 48)
                        if a.after(2):
                            pe.wait_ge(z3, a.k - 1)
                        for q in range(4):
                            last = nc.tensor.transpose(bank[a.slot][:, q * P:(q + 1) * P],
                                                       ain3[:, a.deep, q * P:(q + 1) * P], ident[:, :])
                        last.then_inc(z_ps, 1)
                run_steps(pe, step, before=2, after=1)

            @block.scalar
            def _(act):
                def step(t):
                    if t.exists():
                        act.wait_ge(hz_ps, t.k + 1)
                        if t.after(2):
                            act.wait_ge(o_ps, t.k - 1)
                        nc.scalar.activation(hd[:, t.slot, :], bank[2 + t.slot][:, :], ACT.Tanh,
                                             bias=b1c[:, 1:2]).then_inc(hz3, 1)
                    a = t.plus(-3)
                    if a.exists():
                        act.wait_ge(rstd3, a.k + 1)
                        if a.after(2):
                            act.wait_ge(h_out[a.slot], (a.turn - 1) * 16)
                        for r in range(ACT_ROWS):
                            one = slice(r * D, (r + 1) * D)
                            last = nc.scalar.activation(fin[:, a.slot, one], xc[:, a.four, one], ACT.Copy,
                                                        scale=rstd[:, a.slot, r:r + 1])
                        last.then_inc(fin3, 1)
                    a = t.plus(-1)
                    if a.exists():
                        act.wait_ge(xc3, a.k + 1)
                        if a.after(2):
                            act.wait_ge(ss3, a.k - 1)
                        nc.scalar.activation(sq[:, a.slot, :], xc[:, a.four, :], ACT.Square).then_inc(sq3, 1)
                run_steps(act, step, after=3)

            @block.vector
            def _(dve):
                def step(t):
                    a = t.plus(1)
                    if a.exists():
                        dve.wait_ge(z_ps, a.k + 1)
                        dve.wait_ge(in3[a.deep], a.deep_turn * 48)
                        if a.after(2):
                            dve.wait_ge(hz_ps, a.k - 1)
                        nc.vector.tensor_tensor(ydT[:, a.slot, :], bank[a.slot][:, :], tin3[:, a.deep, :],
                                                ALU.add).then_inc(z3, 1)
                    a = t.plus(-1)
                    if a.exists():
                        dve.wait_ge(o_ps, a.k + 1)
                        if a.after(2):
                            dve.wait_ge(xc3, a.k - 1)
                        nc.vector.tensor_tensor(res[:, a.slot, :], bank[4 + a.slot][:, :], xin3[:, a.deep, :],
                                                ALU.add).then_inc(res3, 1)
                        row_sums(dve, a, res3, rs3)
                    b = t.plus(-2)
                    if b.exists():
                        square_sums(dve, b, sq3, ss3)
                    if a.exists():
                        row_means(dve, a, rs3, mean3, xc3)
                    c = t.plus(-3)
                    if c.exists():
                        dve.wait_ge(rstd3, c.k + 1)
                        if c.after(2):
                            dve.wait_ge(h_out[c.slot], (c.turn - 1) * 16)
                        nc.vector.tensor_tensor(by_row(fin[:, c.slot, :])[:, ACT_ROWS:, :],
                                                by_row(xc[:, c.four, :])[:, ACT_ROWS:, :],
                                                rstd[:, c.slot, ACT_ROWS:].unsqueeze(2)
                                                .to_broadcast([P, ROWS - ACT_ROWS, D]), ALU.mult).then_inc(rest3, 1)
                    if b.exists():
                        row_variances(dve, b, ss3, veps3, rstd3)
                run_steps(dve, step, before=1, after=3)

            @block.gpsimd
            def _(pool):
                def step(t):
                    a = t.plus(-1)
                    if a.exists():
                        centre(pool, a, mean3, sq3, (fin3, rest3), xc3)
                    a = t.plus(-2)
                    if a.exists():
                        pool.wait_ge(veps3, a.k + 1)
                        if a.after(2):
                            for done in (fin3, rest3):
                                pool.wait_ge(done, a.k - 1)
                        nc.gpsimd.tensor_tensor(rstd[:, a.slot, :], veps[:, a.four, :], mhalf[:, :],
                                                ALU.pow).then_inc(rstd3, 1)
                run_steps(pool, step, after=2)

        he_in, h_in, hT_out = ring("he_in", DEEP), ring("h_in", 2), ring("hT_out", 2)
        hT_ps, hT4 = sem("hT_ps"), sem("hT4")
        (gidx4, cnt4, move4, sidx4, heT_ps, heT4, hid_ps, hid4, m_ps, pre4, m4, eq4, sums4, v4, addedm) = (
            sem(n) for n in ("gidx4", "cnt4", "move4", "sidx4", "heT_ps", "heT4", "hid_ps", "hid4", "m_ps", "pre4",
                             "m4", "eq4", "sums4", "v4", "addedm"))

        with nc.Block() as block:
            @block.sync
            def _(sp):
                def step(t):
                    a = t.plus(1)
                    if a.exists():
                        if a.after(2):
                            sp.wait_ge(eq4, a.k - 1)
                            sp.wait_ge(hT_ps, a.k - 1)
                        sp.dma_start(rowbc[:, a.slot, :], group_rows(rows_src, a)).then_inc(rows_in[a.slot], 16)
                        sp.dma_start(xin[:, a.slot, :], chunk_of(h, a)).then_inc(h_in[a.slot], 16)
                    a = t.plus(-1)
                    if a.exists():
                        sp.wait_ge(hT4, a.k + 1)
                        sp.dma_start(hT[bass.ds(a.k, 1), :, :].rearrange("o p n -> (o p) n"),
                                     x1o[:, a.slot, :]).then_inc(hT_out[a.slot], 16)
                run_steps(sp, step, before=1, after=1)
                for s in range(2):
                    sp.wait_ge(hT_out[s], 16 * STEPS // 2)

            @block.gpsimd
            def _(pool):
                def step(t):
                    a = t.plus(GATHER_LEAD)
                    if a.exists():
                        pool.wait_ge(gidx4, 2 * a.k + 2)
                        if a.after(DEEP):
                            pool.wait_ge(heT_ps, a.k - DEEP + 1)
                        gather_group(pool, a, h, he[:, a.deep, :, 0:D], 0, he_in[a.deep])
                        gather_group(pool, a, h, he[:, a.deep, :, D:2 * D], 1, he_in[a.deep])
                    a = t.plus(-ADD_LAG)
                    if a.exists():
                        add_group(pool, a, msum, v4, sidx4, addedm, [(cleared, 32 * STEPS)])
                run_steps(pool, step, before=GATHER_LEAD, after=ADD_LAG)
                pool.wait_ge(addedm, 16 * TILES)

            @block.scalar
            def _(act):
                def step(t):
                    a = t.plus(GATHER_LEAD)
                    if a.exists():
                        if a.after(DEEP):
                            act.wait_ge(he_in[a.deep], (a.deep_turn - 1) * (32 * G))
                        for m, n in enumerate("sd"):
                            nc.scalar.copy(gidx[:, a.deep, m, :], tiles(gat[n], a)).then_inc(gidx4, 1)
                    if t.exists():
                        act.wait_ge(hid_ps, t.k + 1)
                        if t.after(2):
                            act.wait_ge(m_ps, t.k - 1)
                        nc.scalar.activation(hidE[:, t.slot, :], bank[2 + t.slot][:, 0:G * P], ACT.Relu,
                                             bias=eb1c[:, 0:1]).then_inc(hid4, 1)
                    a = t.plus(-1)
                    if a.exists():
                        act.wait_ge(pre4, a.k + 1)
                        if a.after(2):
                            act.wait_ge(sums4, a.k - 1)
                        nc.scalar.activation(x1e[:, a.slot, :, :], pre[:, a.slot, :, :], ACT.Relu).then_inc(m4, 1)
                    a = t.plus(-2)
                    if a.exists():
                        act.wait_ge(sums4, a.k + 1)
                        if a.after(FOUR):
                            act.wait_ge(addedm, (a.k - FOUR + 1) * (16 * G))
                        nc.scalar.copy(vout[:, a.four, :, :], bank[6][:, 0:P]
                                       .rearrange("p (t d) -> p t d", d=D)).then_inc(v4, 1)
                    if t.exists():
                        act.wait_ge(hT_ps, t.k + 1)
                        if t.after(2):
                            act.wait_ge(hT_out[t.slot], (t.turn - 1) * 16)
                        nc.scalar.copy(x1o[:, t.slot, :], bank[5][:, :]).then_inc(hT4, 1)
                run_steps(act, step, before=GATHER_LEAD, after=2)

            @block.vector
            def _(dve):
                def step(t):
                    a = t.plus(1)
                    if a.exists():
                        dve.wait_ge(heT_ps, a.k + 1)
                        if a.after(2):
                            dve.wait_ge(hid_ps, a.k - 1)
                        nc.vector.tensor_copy(heT[:, a.slot, :], bank[a.slot][:, 0:G * P]).then_inc(heT4, 1)
                    a = t.plus(-1)
                    if a.exists():
                        dve.wait_ge(m_ps, a.k + 1)
                        if a.after(2):
                            dve.wait_ge(m4, a.k - 1)
                        nc.vector.tensor_tensor(pre[:, a.slot, :, :], bank[4][:, 0:P]
                                                .rearrange("p (t d) -> p t d", d=D),
                                                eb2r[:, :].unsqueeze(1).to_broadcast([P, G, D]), ALU.add).then_inc(pre4, 1)
                        dve.wait_ge(rows_in[a.slot], (2 * (STEPS // 2) + a.turn) * 16)
                        scatter_rows(dve, a, "s", cnt4, move4)
                        if a.after(FOUR):
                            dve.wait_ge(addedm, (a.k - FOUR + 1) * (16 * G))
                        nc.vector.tensor_tensor(sidx[:, a.four, :], move[:, a.slot, :], tiles(col["s"], a),
                                                ALU.add).then_inc(sidx4, 1)
                        equal_pairs(dve, a, "s", sums4, eq4)
                run_steps(dve, step, before=1, after=1)

            @block.tensor
            def _(pe):
                def step(t):
                    a = t.plus(1)
                    if a.exists():
                        pe.wait_ge(he_in[a.deep], a.deep_turn * (32 * G))
                        if a.after(2):
                            pe.wait_ge(heT4, a.k - 1)
                        for j in range(G):
                            last = nc.tensor.transpose(bank[a.slot][:, j * P:(j + 1) * P], he[:, a.deep, j, :],
                                                       ident[:, :])
                        last.then_inc(heT_ps, 1)
                    a = t.plus(-1)
                    if a.exists():
                        pe.wait_ge(hid4, a.k + 1)
                        if a.after(1):
                            pe.wait_ge(pre4, a.k)
                        for j in range(G):
                            last = nc.tensor.matmul(bank[4][:, j * D:(j + 1) * D],
                                                    hidE[:, a.slot, j * P:(j + 1) * P], ew2[:, :], start=True, stop=True)
                        last.then_inc(m_ps, 1)
                    if t.exists():
                        pe.wait_ge(heT4, t.k + 1)
                        if t.after(2):
                            pe.wait_ge(hid4, t.k - 1)
                        nc.tensor.matmul(bank[2 + t.slot][:, 0:G * P], ew1[:, :], heT[:, t.slot, :],
                                         start=True, stop=True).then_inc(hid_ps, 1)
                    a = t.plus(-2)
                    if a.exists():
                        pe.wait_ge(eq4, a.k + 1)
                        pe.wait_ge(m4, a.k + 1)
                        if a.after(1):
                            pe.wait_ge(v4, a.k)
                        group_sums(a, bank[6], x1e[:, a.slot, :, :]).then_inc(sums4, 1)
                    if t.exists():
                        pe.wait_ge(h_in[t.slot], t.turn * 16)
                        if t.after(1):
                            pe.wait_ge(hT4, t.k)
                        for q in range(4):
                            last = nc.tensor.transpose(bank[5][:, q * P:(q + 1) * P],
                                                       xin[:, t.slot, q * P:(q + 1) * P], ident[:, :])
                        last.then_inc(hT_ps, 1)
                run_steps(pe, step, before=1, after=2)

        in5, y_out = ring("in5", DEEP), ring("y_out", 2)
        hmT5, hn_ps, hn5 = ring("hmT5", 2), ring("hn_ps", 2), ring("hn5", 2)
        (mT_ps, newton, base5, on_ps, std5, res5, rs5, mean5, xc5, sq5, ss5, veps5, rstd5, fin5) = (
            sem(n) for n in ("mT_ps", "newton", "base5", "on_ps", "std5", "res5", "rs5", "mean5", "xc5", "sq5",
                             "ss5", "veps5", "rstd5",
                             "fin5"))

        def refine(dve, a, part):
            if not a.exists():
                return
            r = root[:, a.slot, :]
            if part == 0:
                dve.wait_ge(std5, a.k + 1)
                nc.vector.reciprocal(r, std[:, a.slot, :]).then_inc(newton, 1)
            elif part == 1:
                dve.wait_ge(newton, a.k * 3 + 1)
                nc.vector.tensor_tensor(square[:, a.slot, :], r, r, ALU.mult).then_inc(newton, 1)
            elif part == 2:
                dve.wait_ge(newton, a.k * 3 + 2)
                nc.vector.scalar_tensor_tensor(out=factor[:, a.slot, :], in0=square[:, a.slot, :], scalar=-0.5,
                                               in1=veps[:, a.four, :], op0=ALU.mult, op1=ALU.mult).then_inc(newton, 1)
            else:
                dve.wait_ge(newton, a.k * 3 + 3)
                if a.after(2):
                    dve.wait_ge(fin5, a.k - 1)
                nc.vector.scalar_tensor_tensor(out=rstd[:, a.slot, :], in0=factor[:, a.slot, :], scalar=1.5,
                                               in1=r, op0=ALU.add, op1=ALU.mult).then_inc(rstd5, 1)

        with nc.Block() as block:
            @block.sync
            def _(sp):
                def step(t):
                    a = t.plus(LEAD)
                    if a.exists():
                        if a.after(DEEP):
                            sp.wait_ge(hn_ps[1], a.k - DEEP + 1)
                            sp.wait_ge(base5, a.k - DEEP + 1)
                        sp.dma_start(ain[:, a.deep, :], chunk_of(msum, a)).then_inc(in5[a.deep], 16)
                        for half in range(2):
                            to, of = slice(half * D, (half + 1) * D), slice((1 - half) * D, (2 - half) * D)
                            sp.dma_start(hmT[to, a.deep, half * 512:(half + 1) * 512],
                                         hT[bass.ds(a.k, 1), of, :].rearrange("o p n -> (o p) n")).then_inc(in5[a.deep], 16)
                        sp.dma_start(xin[:, a.deep, :], chunk_of(h, a)).then_inc(in5[a.deep], 16)
                    a = t.plus(-3)
                    if a.exists():
                        store_chunk(sp, a, out, (fin5,), y_out)
                run_steps(sp, step, before=LEAD, after=3)
                for s in range(2):
                    sp.wait_ge(y_out[s], 16 * STEPS // 2)

            @block.tensor
            def _(pe):
                def step(t):
                    a = t.plus(1)
                    if a.exists():
                        pe.wait_ge(in5[a.deep], a.deep_turn * 64)
                        if a.after(2):
                            for half in range(2):
                                pe.wait_ge(hmT5[half], a.k - 1)
                        for q in range(4):
                            last = nc.tensor.transpose(bank[a.slot][:, q * P:(q + 1) * P],
                                                       ain[:, a.deep, q * P:(q + 1) * P], ident[:, :])
                        last.then_inc(mT_ps, 1)
                    if t.exists():
                        for half, weights in enumerate((nw1, nw1s)):
                            pe.wait_ge(hmT5[half], t.k + 1)
                            if t.after(1):
                                pe.wait_ge(hn5[half], t.k)
                            nc.tensor.matmul(bank[2 + half][:, :], weights[:, :],
                                             hmT[:, t.deep, half * 512:(half + 1) * 512],
                                             start=True, stop=True).then_inc(hn_ps[half], 1)
                    a = t.plus(-1)
                    if a.exists():
                        for half in range(2):
                            pe.wait_ge(hn5[half], a.k + 1)
                        if a.after(2):
                            pe.wait_ge(res5, a.k - 1)
                        for r in range(ROWS):
                            place = (1 - r % 2) * 512 + r // 2 * P
                            last = nc.tensor.matmul(bank[4 + a.slot][:, r * D:(r + 1) * D],
                                                    hidN[:, a.slot, place:place + P], nw2[:, :],
                                                    start=True, stop=True)
                        last.then_inc(on_ps, 1)
                run_steps(pe, step, before=1, after=1)

            def spread(act, a, half):
                act.wait_ge(mT_ps, a.k + 1)
                of = slice((1 - half) * D, (2 - half) * D)
                nc.scalar.copy(hmT[of, a.deep, half * 512:(half + 1) * 512], bank[a.slot][of, :]).then_inc(hmT5[half], 1)

            @block.scalar
            def _(act):
                def step(t):
                    a = t.plus(1)
                    if a.exists():
                        for half in range(2):
                            spread(act, a, half)
                    if t.exists():
                        for half in range(2):
                            act.wait_ge(hn_ps[half], t.k + 1)
                            if t.after(2):
                                act.wait_ge(on_ps, t.k - 1)
                            nc.scalar.activation(hidN[:, t.slot, half * 512:(half + 1) * 512], bank[2 + half][:, :],
                                                 ACT.Relu, bias=nb1c[:, 0:1]).then_inc(hn5[half], 1)
                    a = t.plus(-3)
                    if a.exists():
                        act.wait_ge(veps5, a.k + 1)
                        if a.after(2):
                            act.wait_ge(rstd5, a.k - 1)
                        nc.scalar.activation(std[:, a.slot, :], veps[:, a.four, :], ACT.Sqrt).then_inc(std5, 1)
                    a = t.plus(-2)
                    if a.exists():
                        act.wait_ge(xc5, a.k + 1)
                        if a.after(2):
                            act.wait_ge(ss5, a.k - 1)
                        nc.scalar.activation(sq[:, a.slot, :], xc[:, a.four, :], ACT.Square).then_inc(sq5, 1)
                run_steps(act, step, before=1, after=3)

            @block.vector
            def _(dve):
                def step(t):
                    a, b, c = t.plus(-1), t.plus(-2), t.plus(-3)
                    if a.exists():
                        dve.wait_ge(on_ps, a.k + 1)
                        dve.wait_ge(base5, a.k + 1)
                        if a.after(2):
                            dve.wait_ge(xc5, a.k - 1)
                        nc.vector.tensor_tensor(res[:, a.slot, :], base[:, a.slot, :], bank[4 + a.slot][:, :],
                                                ALU.add).then_inc(res5, 1)
                    refine(dve, c, 0)
                    if a.exists():
                        row_sums(dve, a, res5, rs5)
                    refine(dve, c, 1)
                    if b.exists():
                        square_sums(dve, b, sq5, ss5)
                    if a.exists():
                        row_means(dve, a, rs5, mean5, xc5)
                    refine(dve, c, 2)
                    if t.exists():
                        dve.wait_ge(in5[t.deep], t.deep_turn * 64)
                        if t.after(2):
                            dve.wait_ge(res5, t.k - 1)
                        nc.vector.scalar_tensor_tensor(
                            out=by_row(base[:, t.slot, :]), in0=by_row(xin[:, t.deep, :]), scalar=2.0,
                            in1=nb2r[:, :].unsqueeze(1).to_broadcast([P, ROWS, D]),
                            op0=ALU.mult, op1=ALU.add).then_inc(base5, 1)
                    if b.exists():
                        row_variances(dve, b, ss5, veps5, rstd5)
                    refine(dve, c, 3)
                run_steps(dve, step, before=1, after=3)

            @block.gpsimd
            def _(pool):
                def step(t):
                    a = t.plus(-1)
                    if a.exists():
                        centre(pool, a, mean5, sq5, (fin5,), xc5)
                    a = t.plus(-3)
                    if a.exists():
                        pool.wait_ge(rstd5, a.k + 1)
                        if a.after(2):
                            pool.wait_ge(y_out[a.slot], (a.turn - 1) * 16)
                        nc.gpsimd.tensor_tensor(by_row(fin[:, a.slot, :]), by_row(xc[:, a.four, :]),
                                                wide(rstd[:, a.slot, :]), ALU.mult).then_inc(fin5, 1)
                run_steps(pool, step, after=3)


_INS = ['x', 'src', 'dst', 'L0_gnn_W1', 'L0_gnn_b1', 'L0_gnn_W2', 'L0_gnn_b2', 'L1_gnn_eW1', 'L1_gnn_eb1',
        'L1_gnn_eW2', 'L1_gnn_eb2', 'L1_gnn_nW1', 'L1_gnn_nb1', 'L1_gnn_nW2', 'L1_gnn_nb2']


def kernel(**inputs):
    import numpy as _np
    import concourse.bacc as _bacc
    from concourse import mybir as _mybir
    from concourse.bass_utils import run_bass_kernel_spmd as _run

    nc = _bacc.Bacc("TRN2", target_bir_lowering=False, num_devices=1)
    arrays, args = {}, []
    for name in _INS:
        a = _np.ascontiguousarray(inputs[name])
        arrays[f"in_{name}_dram"] = a
        args.append(nc.dram_tensor(f"in_{name}_dram", a.shape, _mybir.dt.from_np(a.dtype), kind="ExternalInput").ap())
    args.append(nc.dram_tensor("out_0_dram", (100000, 64), _mybir.dt.float32, kind="ExternalOutput").ap())
    gnn_kernel(nc, *args)
    r = _run(nc, [arrays], core_ids=[0])
    return r.results[0]["out_0_dram"]
```
